# Optimizing a Trainium2 kernel written in Bass

```python
import numpy as np
import jax
import jax.numpy as jnp

def _softmax(x, axis=-1):
    return jax.nn.softmax(x, axis=axis)

def _gelu(x):
    return jax.nn.gelu(x, approximate=True)

def _silu(x):
    return jax.nn.silu(x)

def _sigmoid(x):
    return jax.nn.sigmoid(x)

def _layernorm(x, axis=-1, eps=1e-05):
    m = jnp.mean(x, axis=axis, keepdims=True)
    v = jnp.var(x, axis=axis, keepdims=True)
    return (x - m) / jnp.sqrt(v + eps)

def _scatter_add(tgt, idx, src, axis=0):
    return tgt.at[idx].add(src)

def _segment_sum(src, seg, n):
    return jax.ops.segment_sum(src, seg, n)
kernel_name = 'mk_recurrent_d1_jaxref_r4_062429'

def setup_inputs(seed: int=0):
    np.random.seed(seed)
    _w = jnp.asarray

    def _L0_attn_setup():
        import jax, jax.numpy as jnp
        import numpy as np
        DIM = 256
        NUM_HEADS = 16
        DIM_HEAD = DIM // NUM_HEADS
        NORM = DIM_HEAD ** (-0.5)
        key = jax.random.key(seed)
        k0, k1, k2, k3 = jax.random.split(key, 4)
        B, N = (2, 512)
        x = jax.random.normal(k0, (B, N, DIM), dtype=jnp.float32)
        Wq = jax.random.normal(k1, (NUM_HEADS, DIM_HEAD, DIM_HEAD), dtype=jnp.float32) * DIM_HEAD ** (-0.5)
        Wp = jax.random.normal(k2, (DIM, DIM), dtype=jnp.float32) * DIM ** (-0.5)
        bp = jax.random.normal(k3, (DIM,), dtype=jnp.float32) * 0.01
        return {'x': x, 'Wq': Wq, 'Wp': Wp, 'bp': bp}
    _L0_attn_in = _L0_attn_setup()

    def _L0_ffn_setup():
        import jax, jax.numpy as jnp
        import numpy as np
        import math
        BETA = 0.9
        THRESHOLD = 1.0
        NUM_STEPS = 5
        ALPHA = 2.0

        @jax.custom_vjp
        def spike_fn(u):
            return (u > 0).astype(u.dtype)

        def _spike_fwd(u):
            return (spike_fn(u), u)

        def _spike_bwd(u, g):
            s = jnp.pi / 2.0 * ALPHA * u
            return (g * (ALPHA / 2.0) / (1.0 + s * s),)
        spike_fn.defvjp(_spike_fwd, _spike_bwd)
        key = jax.random.key(seed)
        k1, k2, k3 = jax.random.split(key, 3)
        n_embd = 256
        x = jax.random.normal(k1, (4, 512, n_embd), dtype=jnp.float32)
        W_fc = jax.random.normal(k2, (4 * n_embd, n_embd), dtype=jnp.float32) / math.sqrt(n_embd)
        W_proj = jax.random.normal(k3, (n_embd, 4 * n_embd), dtype=jnp.float32) / math.sqrt(4 * n_embd)
        return {'x': x, 'W_fc': W_fc, 'W_proj': W_proj}
    _L0_ffn_in = _L0_ffn_setup()
    _d = {'L0_attn_x': _L0_attn_in['x'], 'L0_attn_Wq': _L0_attn_in['Wq'], 'L0_attn_Wp': _L0_attn_in['Wp'], 'L0_attn_bp': _L0_attn_in['bp'], 'L0_ffn_W_fc': _L0_ffn_in['W_fc'], 'L0_ffn_W_proj': _L0_ffn_in['W_proj']}
    _x0 = _d['L0_attn_x']
    _d['L0_attn_x'] = jax.random.normal(jax.random.fold_in(jax.random.key(seed), 1), (16, 1024, 256), dtype=_x0.dtype)
    del _x0
    return _d

def reference(L0_attn_x, L0_attn_Wq, L0_attn_Wp, L0_attn_bp, L0_ffn_W_fc, L0_ffn_W_proj):

    def _L0_attn_ref(x, Wq, Wp, bp):
        import jax, jax.numpy as jnp
        import numpy as np
        DIM = 256
        NUM_HEADS = 16
        DIM_HEAD = DIM // NUM_HEADS
        NORM = DIM_HEAD ** (-0.5)
        B, N, D = x.shape
        xh = x.reshape(B, N, NUM_HEADS, DIM_HEAD)
        q = jnp.einsum('bnhd,hed->bnhe', xh, Wq)
        scores = jnp.einsum('bnhe,bmhe->bhnm', q, q)
        scores = scores / NORM
        attn = jax.nn.softmax(scores, axis=-1)
        res = jnp.einsum('bhnm,bmhe->bnhe', attn, q)
        y = res.reshape(B, N, D)
        y = y @ Wp.T + bp
        return y

    def _L0_ffn_ref(x, W_fc, W_proj):
        import jax, jax.numpy as jnp
        import numpy as np
        import math
        BETA = 0.9
        THRESHOLD = 1.0
        NUM_STEPS = 5
        ALPHA = 2.0

        @jax.custom_vjp
        def spike_fn(u):
            return (u > 0).astype(u.dtype)

        def _spike_fwd(u):
            return (spike_fn(u), u)

        def _spike_bwd(u, g):
            s = jnp.pi / 2.0 * ALPHA * u
            return (g * (ALPHA / 2.0) / (1.0 + s * s),)
        spike_fn.defvjp(_spike_fwd, _spike_bwd)
        h = jnp.square(jax.nn.relu(jnp.einsum('bsd,fd->bsf', x, W_fc)))
        y = jnp.einsum('bsf,df->bsd', h, W_proj)

        def step(mem, _):
            reset = jax.lax.stop_gradient(spike_fn(mem - THRESHOLD))
            mem_new = BETA * mem + y - reset * THRESHOLD
            spk = spike_fn(mem_new - THRESHOLD)
            return (mem_new, spk)
        mem0 = jnp.zeros_like(y)
        _, spks = jax.lax.scan(step, mem0, None, length=NUM_STEPS)
        return jnp.sum(spks, axis=0) / NUM_STEPS
    x = L0_attn_x
    xn = _layernorm(x, axis=-1)
    s = _L0_attn_ref(xn, L0_attn_Wq, L0_attn_Wp, L0_attn_bp)
    g = _silu(_L0_ffn_ref(xn, L0_ffn_W_fc, L0_ffn_W_proj))
    x = x + s * g
    return x

_drawn_inputs = setup_inputs


def setup_inputs(seed=0):
    import zlib

    import numpy as np

    out = dict(_drawn_inputs(seed))
    spreads = {}
    factors = {'L0_attn_bp': 8.0}
    for name, (base, spread) in spreads.items():
        noise = np.random.default_rng([zlib.crc32(name.encode()), seed]).standard_normal(out[name].shape)
        drawn = base * np.exp(spread * noise) if base else spread * noise
        out[name] = jnp.asarray(drawn.astype(out[name].dtype))
    for name, factor in factors.items():
        out[name] = (out[name] * factor).astype(out[name].dtype)
    return out
```

```python
from contextlib import ExitStack

import concourse.bass as bass
from concourse import mybir

FP32 = mybir.dt.float32
FP16 = mybir.dt.float16
BF16 = mybir.dt.bfloat16
INT32 = mybir.dt.int32
ALU = mybir.AluOpType
ACT = mybir.ActivationFunctionType
AX = mybir.AxisListType

B, N, D = 16, 1024, 256
H, DH = 16, 16
F = 4 * D
P = 128
TT = N // P
KD = D // P
KF = F // P
HALF = 512
NH = N // HALF
G = 4
NG = H // G
UNITS = NH * NG
STEPS = UNITS * TT
STRIP = P // G
LN_EPS = 1e-5
BETA, THRESHOLD, SPIKE_STEPS = 0.9, 1.0, 5

QS = 1024.0
SCORE_SCALE = 4.0 / (QS * QS)
CROW = 4096.0
SHIFT = 15.5
R2MAX = 130.0


def spike_thresholds():
    import numpy as np

    def count(y):
        mem, spikes = np.float32(0), 0
        for _ in range(SPIKE_STEPS):
            reset = np.float32(mem - np.float32(THRESHOLD) > 0)
            mem = np.float32(np.float32(np.float32(BETA) * mem) + y) - reset * np.float32(THRESHOLD)
            spikes += int(mem - np.float32(THRESHOLD) > 0)
        return spikes

    found = []
    for k in range(1, SPIKE_STEPS + 1):
        low, high = 0, int(np.float32(64.0).view(np.int32))
        while high - low > 1:
            mid = (low + high) // 2
            low, high = (low, mid) if count(np.int32(mid).view(np.float32)) >= k else (mid, high)
        found.append(float(np.int32(high).view(np.float32)))
    return found


FC, Y, PROJ, XT, Q, C, V = "fc", "y", "proj", "xt", "q", "c", "v"
COST = {FC: 1.75, Y: 6.9, PROJ: 1.8, XT: 0.35, Q: 0.9, C: 0.45, V: 1.0}
COUNT = {FC: KF * NH, Y: TT // 2, PROJ: TT // 2, XT: KD * NH, Q: KD * NH, C: NH, V: TT // 2}
OWN_A = [(FC, k) for k in range(8)] + [(Y, k) for k in range(2)] + [(FC, k) for k in range(8, 16)] \
    + [(PROJ, k) for k in range(2)]
PREP = [(XT, k) for k in range(4)] + [(Q, k) for k in range(4)] + [(C, k) for k in range(2)] \
    + [(V, k) for k in range(4)]
OWN_B = [(Y, k) for k in range(2, 4)]
TAIL = [(PROJ, k) for k in range(2, 4)]
LAST_STEP = STEPS - 3


def prep_groups(exact):
    return [group for group in PREP if not (exact and group[0] == C)]


def schedule(prep):
    order = OWN_A + prep + OWN_B
    parts = {FC: 2, Y: 16, PROJ: 4, XT: 1, Q: 1, C: 1, V: 1}
    pieces = [(kind, k, part, parts[kind], n) for n, (kind, k) in enumerate(order) for part in range(parts[kind])]
    total = sum(COST[kind] for kind, _ in order)
    at, out, done = 0.0, [[] for _ in range(STEPS)], {}
    for piece in pieces:
        kind = piece[0]
        step = int(at / total * LAST_STEP)
        if kind == PROJ:
            step = max(step, STEPS // 2 + 3)
        step = max(step, max(done.values(), default=0))
        step = min(step, LAST_STEP)
        out[step].append(piece)
        done[(kind, piece[1])] = step
        at += COST[kind] / parts[kind]
    return out, done


class Signals:

    def __init__(self, sem, way):
        self.x_in = sem(f"{way}_x_in")
        self.x_again = sem(f"{way}_x_again")
        self.out_done = sem(f"{way}_out_done")
        self.q_out = sem(f"{way}_q_out")
        self.c_out = sem(f"{way}_c_out")
        self.scored = sem(f"{way}_scored")
        self.pv_done = sem(f"{way}_pv_done")
        self.exp_done = sem(f"{way}_exp_done")
        self.xnt_set = sem(f"{way}_xnt_set")
        self.v_staged = sem(f"{way}_v_staged")
        self.y_set = sem(f"{way}_y_set")
        self.th_set = sem(f"{way}_th_set")
        self.stat_set = sem(f"{way}_stat_set")
        self.aggr_set = sem(f"{way}_aggr_set")
        self.xn_set = sem(f"{way}_xn_set")
        self.relu_set = sem(f"{way}_relu_set")
        self.qhi_set = sem(f"{way}_qhi_set")
        self.qlo_set = sem(f"{way}_qlo_set")
        self.c_set = sem(f"{way}_c_set")
        self.min_set = sem(f"{way}_min_set")
        self.cnt_link = sem(f"{way}_cnt_link")
        self.gate_set = sem(f"{way}_gate_set")
        self.norm_link = sem(f"{way}_norm_link")
        self.res_set = sem(f"{way}_res_set")
        self.s_set = sem(f"{way}_s_set")
        self.comb_link = sem(f"{way}_comb_link")
        self.comb_set = sem(f"{way}_comb_set")
        self.veps_set = sem(f"{way}_veps_set")
        self.rstd_set = sem(f"{way}_rstd_set")
        self.h_set = sem(f"{way}_h_set")
        self.sq_set = sem(f"{way}_sq_set")
        self.vones_set = sem(f"{way}_vones_set")
        self.max_scored = sem(f"{way}_max_scored")
        self.max_set = sem(f"{way}_max_set")
        self.max_t = sem(f"{way}_max_t")
        self.max_out = sem(f"{way}_max_out")
        self.max_in = sem(f"{way}_max_in")
        self.stack_in = [sem(f"{way}_stack_in{g}") for g in range(NG)]
        self.pe_done = {kind: sem(f"{way}_pe_{kind}") for kind in COUNT}


def build(nc, x, wq_t, wp_s, bp, wfc_t, wproj_t, consts, q_scratch, c_scratch, q_own_scratch,
          max_scratch, bound_scratch, out):
    thresholds = spike_thresholds()
    x_v = x.rearrange("b (p t) d -> b p t d", p=P)
    out_v = out.rearrange("b (p t) d -> b p t d", p=P)

    ctx = ExitStack()
    with ctx:
        def sb(name, shape, dtype):
            return ctx.enter_context(nc.sbuf_tensor(name, shape, dtype))

        def sem(name):
            return ctx.enter_context(nc.semaphore(name))

        w_fc = sb("w_fc", [P, KD, F], FP32)
        w_proj = sb("w_proj", [P, KF, D], FP32)
        w_p = sb("w_p", [P, NG // 2, D], FP32)
        w_q = sb("w_q", [P, KD, P], FP32)
        b_p = sb("b_p", [P, D], FP32)
        const = sb("const", [P, P + 2 + KD * H], FP32)
        ident = const[:, 0:P]
        strip_half = [const[:, P + i:P + i + 1] for i in range(2)]
        head_sum = sb("head_sum", [P, KD, H], BF16)
        minus_half = sb("minus_half", [P, TT], FP32)
        x_tok = sb("x_tok", [P, TT, D], FP32)
        stats = sb("stats", [P, TT, 6], FP32)
        mean_var = sb("mean_var", [P, TT, 2], FP32)
        var_eps = sb("var_eps", [P, TT], FP32)
        rstd = sb("rstd", [P, TT], FP32)
        xn_t = sb("xn_t", [P, KD, N], FP32)
        q_hi = sb("q_hi", [P, KD, N], FP16)
        q_lo = sb("q_lo", [P, KD, N], FP16)
        q_sq = sb("q_sq", [P, KD, N], BF16)
        c_row = sb("c_row", [H, N], FP16)
        key_stack = sb("key_stack", [65, H, N], FP16)
        query_stack = sb("query_stack", [65, H, N], FP16)
        v_stage = sb("v_stage", [P, TT, D], FP32)
        v_ones = sb("v_ones", [P, TT, H, STRIP], FP32)
        NE = 4
        e = sb("e", [P, NE, 2, HALF], FP32)
        recip = sb("recip", [P, HALF], FP32)
        recip_b = sb("recip_b", [P, HALF], FP32)
        res = sb("res", [P, NH, NG // 2, HALF], FP32)
        r = sb("r", [P, 2, HALF], FP32)
        h_t = sb("h_t", [P, KF, HALF], FP32)
        y_sb = sb("y_sb", [P, 2, HALF], FP32)
        cnt = sb("cnt", [P, TT // 2, HALF], FP32)
        x_out = sb("x_out", [P, TT // NH, D], FP32)
        s_b = sb("s_b", [P, HALF], FP32)
        c_min = sb("c_min", [H, 2], FP32)
        c_all = sb("c_all", [1, H], FP32)
        flag = sb("flag", [1, 1], INT32)
        q_own = x_tok[:, :, :].rearrange("p t d -> p (t d)").rearrange("p (k n) -> p k n", k=KD)
        q_rows = [stack[:, :, :].bitcast(FP32) for stack in (key_stack, query_stack)]
        pick_max = sb("pick_max", [33, P], FP32)
        row_max = sb("row_max", [P, H, TT], FP32)
        row_max_t = sb("row_max_t", [P, P], FP32)

        scores = [ctx.enter_context(nc.psum_tensor(f"scores{i}", [P, 2, HALF], FP32)) for i in range(2)]
        acc = [ctx.enter_context(nc.psum_tensor(f"acc{i}", [P, HALF], FP32)) for i in range(2)]
        aux = [ctx.enter_context(nc.psum_tensor(f"aux{i}", [P, HALF], FP32)) for i in range(2)]

        w_in, wq_in, w_set, v_set = sem("w_in"), sem("wq_in"), sem("w_set"), sem("v_set")
        flag_part, flag_out, flag_in, flag_set = sem("flag_part"), sem("flag_out"), sem("flag_in"), sem("flag_set")
        cleared = sem("cleared")
        bounded, general = Signals(sem, "bounded"), Signals(sem, "general")

        def wait(eng, semaphore, value):
            if not (isinstance(value, int) and value <= 0):
                eng.wait_ge(semaphore, value)

        def wait_apart(eng, semaphore, value):
            wait(eng, semaphore, value)
            eng.nop(nofuse=True)

        def emptied(s, kind, b, k):
            return {FC: (s.relu_set, b * 16 + (k + 1)), Y: (s.y_set, b * 4 + (k + 1)), PROJ: (s.s_set, b * 4 + (k + 1)),
                    XT: (s.xnt_set, b * 4 + (k + 1)), Q: (s.qlo_set, b * 4 + (k + 1)), C: (s.c_set, b * 2 + (k + 1)),
                    V: (s.v_staged, b * 4 + (k + 1))}[kind]

        block = ctx.enter_context(nc.Block())

        def batches(eng, body, exact):
            body(0, prep_groups(exact))
            with eng.Fori(1, B - 1) as b:
                body(b, prep_groups(exact))
            body(B - 1, [])

        def in_general(eng, run):
            eng.wait_ge(bounded.out_done, B * 32)
            eng.wait_ge(flag_set, 1)
            beyond = eng.value_load(flag[0:1, 0:1], min_val=0, max_val=1)
            with eng.If(beyond > 0):
                run(general, True)

        @block.sync
        def _(sp):
            for dst, src in ((const[:, :], consts), (w_fc[:, :, :], wfc_t), (w_proj[:, :, :], wproj_t),
                             (w_p[:, :, :], wp_s), (b_p[:, :], bp.rearrange("(a d) -> a d", a=1).broadcast_to((P, D)))):
                sp.dma_start(dst, src).then_inc(w_in, 16)
            sp.wait_ge(w_set, 1)
            for h in range(H):
                p = DH * h % P
                sp.dma_start(w_q[p:p + DH, h // 8, p:p + DH], wq_t[h, :, :]).then_inc(wq_in, 16)

            def run(s, exact):
                stack_loads = 16 * (2 if exact else 7)

                def load_x(b):
                    wait_apart(sp, s.pe_done[XT], b * 4)
                    if exact:
                        wait(sp, s.q_out, b * 32)
                    sp.dma_start(x_tok[:, :, :], x_v[b, :, :, :]).then_inc(s.x_in, 16)

                def store_q(b):
                    wait_apart(sp, s.qlo_set, b * 4 + 4)
                    for g in range(NG):
                        wait_apart(sp, s.stack_in[g], b * stack_loads)
                    if exact:
                        for k in range(KD):
                            sp.dma_start(q_own_scratch[8 * k:8 * k + 8, :, :], q_own[:, k, :]).then_inc(s.q_out, 16)
                        wait_apart(sp, s.q_out, b * 32 + 32)
                        return
                    for part, q in enumerate((q_hi, q_lo)):
                        for k in range(KD):
                            sp.dma_start(q_scratch[8 * k:8 * k + 8, part, :, :], q[:, k, :]).then_inc(s.q_out, 16)
                    sp.wait_ge(s.c_set, b * 2 + 2)
                    sp.dma_start(c_scratch, c_row[:, :]).then_inc(s.c_out, 16)
                    wait_apart(sp, s.q_out, b * 64 + 64)
                    wait_apart(sp, s.c_out, b * 16 + 16)

                def load_stack(b, g):
                    wait_apart(sp, s.scored, (b - 1) * 128 + (NG + g + 1) * 16)
                    heads = slice(G * g, G * g + G)
                    if exact:
                        for half in range(NH):
                            sp.dma_start(q_rows[half][0:DH, heads, :],
                                         q_own_scratch[heads, :, half * HALF:(half + 1) * HALF].rearrange("h e n -> e h n")) \
                                .then_inc(s.stack_in[g], 16)
                        return
                    for rep in range(2):
                        sp.dma_start(query_stack[32 * rep:32 * rep + 32, heads, :],
                                     q_scratch[heads, :, :, :].rearrange("h s e n -> (s e) h n")).then_inc(s.stack_in[g], 16)
                        for part in range(2):
                            row = 32 * part + 16 * rep
                            sp.dma_start(key_stack[row:row + 16, heads, :],
                                         q_scratch[heads, part, :, :].rearrange("h e n -> e h n")).then_inc(s.stack_in[g], 16)
                    sp.dma_start(query_stack[64:65, heads, :],
                                 c_scratch[heads, :].rearrange("(a h) n -> a h n", a=1)).then_inc(s.stack_in[g], 16)

                def store_out(b, half):
                    sp.wait_ge(s.comb_set, b * 4 + (2 * half + 2))
                    sp.dma_start(out_v[b, :, 4 * half:4 * half + 4, :], x_out[:, :, :]).then_inc(s.out_done, 16)

                def load_again(b, half):
                    wait(sp, s.out_done, b * 32 + 16 * half)
                    sp.dma_start(x_out[:, :, :], x_v[b, :, 4 * half:4 * half + 4, :]).then_inc(s.x_again, 16)

                def place_max(b):
                    sp.wait_ge(s.max_set, b * 129 + 129)
                    sp.dma_start(max_scratch, row_max_t[:, :]).then_inc(s.max_out, 16)
                    wait_apart(sp, s.max_out, b * 16 + 16)
                    wait(sp, s.scored, b * 128)
                    for half in range(NH):
                        sp.dma_start(q_rows[half][32:33, :, :],
                                     max_scratch.rearrange("(a h s t) n -> s a h (t n)", a=1, h=H, s=NH)[half]).then_inc(s.max_in, 16)

                def collect_bound():
                    sp.wait_ge(s.min_set, B * 2)
                    sp.dma_start(bound_scratch, c_min[:, 0:1]).then_inc(flag_out, 16)
                    sp.wait_ge(flag_out, 16)
                    sp.dma_start(c_all[:, :], bound_scratch.rearrange("h a -> a h")).then_inc(flag_in, 16)

                load_x(0)
                store_q(0)
                if exact:
                    sp.wait_ge(cleared, 4)
                for g in range(NG):
                    load_stack(0, g)

                def body(b, prep):
                    if exact:
                        place_max(b)
                    elif not prep:
                        collect_bound()
                    load_again(b, 0)
                    if prep:
                        load_x(b + 1)
                    store_out(b, 0)
                    load_again(b, 1)
                    if prep:
                        store_q(b + 1)
                        for g in range(NG):
                            load_stack(b + 1, g)
                    store_out(b, 1)

                batches(sp, body, exact)
                sp.wait_ge(s.out_done, B * 32)

            run(bounded, False)
            in_general(sp, run)

        @block.tensor
        def _(pe):
            def run(s, exact):
                def aux_part(b, piece, before):
                    kind, k, part, parts, n = piece
                    bank = aux[n % 2]
                    if part == 0:
                        wait(pe, *before)
                    if kind == FC:
                        half, f = k // KF, k % KF
                        ins = nc.tensor.matmul(bank[:, :], w_fc[:, part, f * P:(f + 1) * P],
                                               xn_t[:, part, half * HALF:(half + 1) * HALF], start=part == 0, stop=part == 1)
                    elif kind == Y:
                        t, f = part // KF, part % KF
                        if part == 0:
                            pe.wait_ge(s.h_set, b * 16 + (8 * (k // 2) + 1))
                        if part < KF:
                            pe.wait_ge(s.h_set, b * 16 + (8 * (k // 2) + f + 1))
                        col = (2 * k + t) % 4 * P
                        ins = nc.tensor.matmul(bank[:, t * D:(t + 1) * D], h_t[:, f, col:col + P], w_proj[:, f, :],
                                               start=f == 0, stop=f == KF - 1)
                    elif kind == PROJ:
                        t, pair = part // 2, part % 2
                        half = k // 2
                        if part == 0:
                            pe.wait_ge(s.res_set, b * 8 + (4 * half + 4))
                        col = (2 * k + t) % 4 * P
                        ins = nc.tensor.matmul(bank[:, t * D:(t + 1) * D], res[:, half, pair, col:col + P], w_p[:, pair, :],
                                               start=pair == 0, stop=pair == 1)
                    elif kind == XT:
                        chunk, half = k % 2, k // 2
                        pe.wait_ge(s.xn_set, b * 8 + (4 * half + 4))
                        for t in range(4):
                            ins = nc.tensor.transpose(bank[:, t * P:(t + 1) * P],
                                                      x_tok[:, 4 * half + t, chunk * P:(chunk + 1) * P], ident)
                    elif kind == Q:
                        chunk, half = k % 2, k // 2
                        pe.wait_ge(s.xnt_set, b * 4 + 4)
                        ins = nc.tensor.matmul(bank[:, :], w_q[:, chunk, :], xn_t[:, chunk, half * HALF:(half + 1) * HALF],
                                               start=True, stop=True)
                    elif kind == C:
                        pe.wait_ge(s.sq_set, b * 4 + (2 * k + 2))
                        for chunk in range(KD):
                            ins = nc.tensor.matmul(bank[0:H, :], head_sum[:, chunk, :], q_sq[:, chunk, k * HALF:(k + 1) * HALF],
                                                   start=chunk == 0, stop=chunk == KD - 1)
                    else:
                        for t in range(2):
                            for chunk in range(KD):
                                ins = nc.tensor.matmul(bank[:, t * D + chunk * P:t * D + (chunk + 1) * P],
                                                       xn_t[:, chunk, (2 * k + t) * P:(2 * k + t + 1) * P],
                                                       w_q[:, chunk, :], start=True, stop=True)
                    if part == parts - 1:
                        ins.then_inc(s.pe_done[kind], 1)

                def pv(b, i):
                    unit, j = i // TT, i % TT
                    half, g = unit // NG, unit % NG
                    if j == 0:
                        wait(pe, s.res_set, b * 8 + (unit - 1))
                        if half == 0:
                            pe.wait_ge(s.vones_set, b * 4 + (g + 1))
                    pe.wait_ge(s.exp_done, b * 128 + (2 * i + 2))
                    for n in range(G):
                        tile = (2 * i + n // 2) % NE
                        ins = nc.tensor.matmul(acc[unit % 2][STRIP * n:STRIP * (n + 1), :], v_ones[:, j, G * g + n, :],
                                               e[:, tile, n % 2, :], start=j == 0, stop=j == TT - 1)
                    ins.then_inc(s.pv_done, 1)

                def row_maxima(b):
                    for g in range(NG):
                        pe.wait_ge(s.stack_in[g], b * 32 + 32)
                    for i in range(H * TT):
                        head, t = i // TT, i % TT
                        if i >= 2:
                            pe.wait_ge(s.max_set, b * 129 + (i - 1))
                        for half in range(NH):
                            ins = nc.tensor.matmul(scores[i % 2][:, half, :],
                                                   q_rows[t // 4][0:DH, head, t % 4 * P:(t % 4 + 1) * P],
                                                   q_rows[half][0:DH, head, :], start=True, stop=True)
                        ins.then_inc(s.max_scored, 1)
                    pe.wait_ge(s.max_set, b * 129 + 128)
                    nc.tensor.transpose(scores[0][:, 0, 0:P], row_max[:, :, :].rearrange("p h t -> p (h t)"), ident) \
                        .then_inc(s.max_t, 1)
                    pe.wait_ge(s.max_in, b * 32 + 32)

                def score(bank, head, half, j):
                    if not exact:
                        return nc.tensor.matmul(bank, key_stack[:, head, j * P:(j + 1) * P],
                                                query_stack[:, head, half * HALF:(half + 1) * HALF], start=True, stop=True)
                    nc.tensor.matmul(bank, q_rows[j // 4][0:DH, head, j % 4 * P:(j % 4 + 1) * P],
                                     q_rows[half][0:DH, head, :], start=True, stop=False)
                    return nc.tensor.matmul(bank, pick_max[:, :], q_rows[half][0:33, head, :], start=False, stop=True)

                pe.wait_ge(w_in, 5 * 16)
                pe.wait_ge(wq_in, H * 16)
                pe.wait_ge(w_set, 4)
                for n, (kind, k) in enumerate(prep_groups(exact)):
                    before = emptied(s, prep_groups(exact)[n - 2][0], 0, prep_groups(exact)[n - 2][1]) if n >= 2 else (w_in, 0)
                    aux_part(0, (kind, k, 0, 1, n), before)
                pe.wait_ge(v_set, 2)
                if exact:
                    pe.wait_ge(cleared, 4)

                def body(b, prep):
                    steps, _ = schedule(prep)
                    order = [(b, kind, k) for kind, k in OWN_A] + ([(b + 1, kind, k) for kind, k in prep]) \
                        + [(b, kind, k) for kind, k in OWN_B + TAIL]
                    if isinstance(b, int) and b == 0:
                        ahead = [(0, V, 2), (0, V, 3)]
                    else:
                        ahead = [(b - 1, PROJ, 2), (b - 1, PROJ, 3)]

                    def before(n):
                        batch, kind, k = (ahead + order)[n]
                        return emptied(s, kind, batch, k)

                    if exact:
                        row_maxima(b)
                    for i in range(STEPS):
                        unit, j = i // TT, i % TT
                        half, g = unit // NG, unit % NG
                        if j == 0 and half == 0 and not exact:
                            pe.wait_ge(s.stack_in[g], b * 112 + 112)
                        for pair in range(2):
                            tile = 2 * i + pair
                            wait(pe, s.exp_done, b * 128 + (tile - 1))
                            for n in range(2):
                                head = G * g + 2 * pair + n
                                ins = score(scores[tile % 2][:, n, :], head, half, j)
                            ins.then_inc(s.scored, 1)
                        if i:
                            pv(b, i - 1)
                        for piece in steps[i]:
                            aux_part(order[piece[4]][0], piece, before(piece[4]))
                    pv(b, STEPS - 1)
                    for n, (kind, k) in enumerate(TAIL):
                        at = len(order) - 2 + n
                        for part in range(4):
                            aux_part(b, (kind, k, part, 4, at), before(at))

                batches(pe, body, exact)

            run(bounded, False)
            in_general(pe, run)

        @block.scalar
        def _(act):
            def run(s, exact):
                def evac(b, kind, k, bank):
                    if kind == XT:
                        chunk, half = k % 2, k // 2
                        wait(act, s.pe_done[FC], b * 16)
                        wait(act, s.pe_done[V], b * 4)
                        act.wait_ge(s.pe_done[XT], b * 4 + (k + 1))
                        nc.scalar.activation(xn_t[:, chunk, half * HALF:(half + 1) * HALF], bank[:, :], ACT.Copy).then_inc(s.xnt_set, 1)
                    elif kind == V:
                        wait(act, s.vones_set, b * 4)
                        act.wait_ge(s.pe_done[V], b * 4 + (k + 1))
                        nc.scalar.activation(v_stage[:, 2 * k:2 * k + 2, :], bank[:, :].rearrange("p (t d) -> p t d", t=2),
                                             ACT.Copy).then_inc(s.v_staged, 1)
                    elif kind == Y:
                        wait(act, s.gate_set, b * 4 + (k - 1))
                        act.wait_ge(s.pe_done[Y], b * 4 + (k + 1))
                        nc.scalar.activation(y_sb[:, k % 2, :], bank[:, :], ACT.Copy).then_inc(s.y_set, 1)

                def tanh(b, k):
                    act.wait_ge(s.cnt_link, b * 20 + (k + 1) * 5)
                    nc.scalar.activation(y_sb[:, k % 2, :], cnt[:, k, :], ACT.Tanh, scale=0.5 / SPIKE_STEPS).then_inc(s.th_set, 1)

                for n, (kind, k) in enumerate(prep_groups(exact)):
                    if kind in (XT, V):
                        evac(0, kind, k, aux[n % 2])

                def body(b, prep):
                    _, done = schedule(prep)
                    order = OWN_A + prep + OWN_B
                    tasks = []
                    for n, (kind, k) in enumerate(order):
                        if kind in (XT, V, Y):
                            tasks.append((done[(kind, k)], n, kind, k))
                        if kind == Y:
                            tasks.append((min(done[(kind, k)] + 4, STEPS), n, "tanh", k))
                    for i in range(STEPS + 1):
                        if i < STEPS:
                            for tile in (2 * i, 2 * i + 1):
                                act.wait_ge(s.scored, b * 128 + (tile + 1))
                                wait(act, s.pv_done, b * 64 + (tile // 2 - NE // 2 + 1))
                                nc.scalar.activation(e[:, tile % NE, :, :], scores[tile % 2][:, :, :], ACT.Exp,
                                                     scale=4.0 if exact else SCORE_SCALE).then_inc(s.exp_done, 1)
                        for at, n, kind, k in sorted(tasks, key=lambda task: (task[0], task[1])):
                            if at == i:
                                if kind == "tanh":
                                    tanh(b, k)
                                else:
                                    evac(b + 1 if kind in (XT, V) else b, kind, k, aux[n % 2])

                batches(act, body, exact)

            run(bounded, False)
            in_general(act, run)

        @block.vector
        def _(dve):
            nc.vector.memset(w_q[:, :, :], 0.0).then_inc(w_set, 1)
            nc.vector.memset(minus_half[:, :], -0.5).then_inc(w_set, 1)
            nc.vector.memset(key_stack[64:65, :, :], CROW).then_inc(w_set, 1)
            dve.wait_ge(w_in, 5 * 16)
            nc.vector.tensor_copy(head_sum[:, :, :], const[:, P + 2:].rearrange("p (k h) -> p k h", k=KD)).then_inc(w_set, 1)
            nc.vector.memset(v_ones[:, :, :, :], 1.0).then_inc(v_set, 1)
            nc.vector.memset(c_min[:, :], 0.0).then_inc(v_set, 1)

            def run(s, exact):
                def ln_stats(b, t):
                    if t == 0:
                        dve.wait_ge(s.x_in, b * 16 + 16)
                        wait(dve, s.xn_set, b * 8)
                    nc.vector.bn_stats(stats[:, t, :], x_tok[:, t, :]).then_inc(s.stat_set, 1)
                    if t == TT - 1:
                        wait_apart(dve, s.rstd_set, b)
                        wait_apart(dve, s.stat_set, b * 8 + 8)
                        for u in range(TT):
                            nc.vector.bn_aggr(mean_var[:, u, :], stats[:, u, :]).then_inc(s.aggr_set, 1)

                def ln_apply(b, t):
                    dve.wait_ge(s.rstd_set, b + 1)
                    nc.vector.tensor_scalar(x_tok[:, t, :], x_tok[:, t, :], mean_var[:, t, 0:1], rstd[:, t:t + 1],
                                            ALU.subtract, ALU.mult).then_inc(s.xn_set, 1)

                def q_split(b, k, bank):
                    chunk, half = k % 2, k // 2
                    cols = slice(half * HALF, (half + 1) * HALF)
                    dve.wait_ge(s.pe_done[Q], b * 4 + (k + 1))
                    if exact:
                        nc.vector.tensor_scalar(q_own[:, chunk, cols], bank[:, :], 1.0, None, ALU.mult).then_inc(s.qlo_set, 1)
                        return
                    wait(dve, s.q_out, b * 64)
                    wait(dve, s.sq_set, b * 4)
                    nc.vector.tensor_scalar(q_hi[:, chunk, cols], bank[:, :], QS, None, ALU.mult).then_inc(s.qhi_set, 1)
                    dve.wait_ge(s.qhi_set, b * 4 + (k + 1))
                    nc.vector.scalar_tensor_tensor(q_lo[:, chunk, cols], bank[:, :], QS, q_hi[:, chunk, cols],
                                                   ALU.mult, ALU.subtract).then_inc(s.qlo_set, 1)

                def c_rows(b, k, bank):
                    dve.wait_ge(s.pe_done[C], b * 2 + (k + 1))
                    wait(dve, s.c_out, b * 16)
                    wait(dve, s.min_set, b * 2)
                    nc.vector.tensor_scalar(c_row[:, k * HALF:(k + 1) * HALF], bank[0:H, :], -1.0 / CROW,
                                            -SHIFT * QS * QS / CROW, ALU.mult, ALU.add).then_inc(s.c_set, 1)
                    if k == NH - 1:
                        dve.wait_ge(s.c_set, b * 2 + 2)
                        nc.vector.tensor_reduce(c_min[:, 1:2], c_row[:, :], AX.X, ALU.min).then_inc(s.min_set, 1)
                        dve.wait_ge(s.min_set, b * 2 + 1)
                        nc.vector.tensor_tensor(c_min[:, 0:1], c_min[:, 0:1], c_min[:, 1:2], ALU.min).then_inc(s.min_set, 1)

                def relu(b, k, bank):
                    dve.wait_ge(s.pe_done[FC], b * 16 + (k + 1))
                    wait(dve, s.h_set, b * 16 + (k - 1))
                    nc.vector.tensor_scalar(r[:, k % 2, :], bank[:, :], 0.0, None, ALU.max).then_inc(s.relu_set, 1)

                def spikes(b, k):
                    dve.wait_ge(s.y_set, b * 4 + (k + 1))
                    wait(dve, s.comb_link, (b - 1) * 4 + k + 1)
                    link = b * 20 + k * 5
                    nc.vector.tensor_scalar(cnt[:, k, :], y_sb[:, k % 2, :], thresholds[0], None, ALU.is_ge).then_inc(s.cnt_link, 1)
                    for n in range(1, SPIKE_STEPS):
                        dve.wait_ge(s.cnt_link, link + n)
                        nc.vector.scalar_tensor_tensor(cnt[:, k, :], y_sb[:, k % 2, :], thresholds[n], cnt[:, k, :],
                                                       ALU.is_ge, ALU.add).then_inc(s.cnt_link, 1)

                def gate(b, k):
                    dve.wait_ge(s.th_set, b * 4 + (k + 1))
                    nc.vector.scalar_tensor_tensor(cnt[:, k, :], y_sb[:, k % 2, :], 1.0, cnt[:, k, :], ALU.add, ALU.mult).then_inc(s.gate_set, 1)

                def normalise(b, unit):
                    half, g = unit // NG, unit % NG
                    a = acc[unit % 2]
                    links = b * 20 + unit // 2 * 5 + (unit % 2) * 2
                    dve.wait_ge(s.pv_done, b * 64 + (unit + 1) * TT)
                    if unit:
                        dve.wait_ge(s.res_set, b * 8 + unit)
                    else:
                        wait(dve, s.res_set, b * 8)
                    nc.vector.reciprocal(recip[:, :], a[:, :]).then_inc(s.norm_link, 1)
                    wait_apart(dve, s.norm_link, links + 1)
                    nc.vector.stream_shuffle(recip_b[:, :], recip[:, :], [16 if g % 2 == 0 else 0] * 32).then_inc(s.norm_link, 1)
                    dve.wait_ge(s.norm_link, links + 2)
                    target = res[:, half, g // 2, :]
                    if g % 2 == 0:
                        wait(dve, s.pe_done[PROJ], (b - 1) * 4 + (2 * half + 2))
                        nc.vector.scalar_tensor_tensor(target, a[:, :], strip_half[0], recip_b[:, :], ALU.mult, ALU.mult).then_inc(s.res_set, 1)
                    else:
                        nc.vector.tensor_tensor(recip[:, :], a[:, :], recip_b[:, :], ALU.mult).then_inc(s.norm_link, 1)
                        dve.wait_ge(s.norm_link, links + 3)
                        nc.vector.scalar_tensor_tensor(target, recip[:, :], strip_half[1], target, ALU.mult, ALU.add).then_inc(s.res_set, 1)

                def combine(b, k, bank):
                    dve.wait_ge(s.pe_done[PROJ], b * 4 + (k + 1))
                    wait(dve, s.comb_set, b * 4 + k)
                    for t in range(2):
                        ins = nc.vector.tensor_tensor(s_b[:, t * D:(t + 1) * D], bank[:, t * D:(t + 1) * D], b_p[:, :], ALU.add)
                    ins.then_inc(s.s_set, 1)
                    dve.wait_ge(s.s_set, b * 4 + (k + 1))
                    dve.wait_ge(s.gate_set, b * 4 + (k + 1))
                    nc.vector.scalar_tensor_tensor(s_b[:, :], s_b[:, :], 0.5 / SPIKE_STEPS, cnt[:, k, :],
                                                   ALU.mult, ALU.mult).then_inc(s.comb_link, 1)
                    dve.wait_ge(s.comb_link, b * 4 + (k + 1))
                    dve.wait_ge(s.x_again, b * 32 + 16 * (k // 2 + 1))
                    tiles = slice(2 * (k % 2), 2 * (k % 2) + 2)
                    nc.vector.tensor_tensor(x_out[:, tiles, :], s_b[:, :].rearrange("p (t d) -> p t d", t=2),
                                            x_out[:, tiles, :], ALU.add).then_inc(s.comb_set, 1)

                def row_maxima(b):
                    wait(dve, s.max_t, b)
                    for i in range(H * TT):
                        dve.wait_ge(s.max_scored, b * 128 + (i + 1))
                        nc.vector.tensor_reduce(row_max[:, i // TT, i % TT:i % TT + 1],
                                                scores[i % 2][:, :, :].rearrange("p a n -> p (a n)"), AX.X, ALU.max) \
                            .then_inc(s.max_set, 1)
                    dve.wait_ge(s.max_t, b + 1)
                    wait(dve, s.max_out, b * 16)
                    nc.vector.tensor_scalar(row_max_t[:, :], scores[0][:, 0, 0:P], -1.0, None, ALU.mult).then_inc(s.max_set, 1)

                def set_flag():
                    dve.wait_ge(flag_in, 16)
                    nc.vector.tensor_reduce(c_all[0:1, 0:1], c_all[:, :], AX.X, ALU.min).then_inc(flag_part, 1)
                    dve.wait_ge(flag_part, 1)
                    nc.vector.tensor_scalar(flag[:, :], c_all[0:1, 0:1], -(R2MAX + SHIFT) * QS * QS / CROW, None, ALU.is_lt) \
                        .then_inc(flag_set, 1)

                if exact:
                    for stack in q_rows:
                        nc.vector.memset(stack[0:33, :, :], 0.0).then_inc(cleared, 1)
                    nc.vector.memset(pick_max[:, :], 0.0).then_inc(cleared, 1)
                    dve.wait_ge(cleared, 3)
                    nc.vector.memset(pick_max[32:33, :], 1.0).then_inc(cleared, 1)
                for t in range(TT):
                    ln_stats(0, t)
                for t in range(TT):
                    ln_apply(0, t)
                for n, (kind, k) in enumerate(prep_groups(exact)):
                    if kind == Q:
                        q_split(0, k, aux[n % 2])
                    if kind == C:
                        c_rows(0, k, aux[n % 2])

                def body(b, prep):
                    if exact:
                        row_maxima(b)
                    _, done = schedule(prep)
                    order = OWN_A + prep + OWN_B
                    tasks = []
                    for n, (kind, k) in enumerate(order):
                        at, bank = done[(kind, k)], aux[n % 2]
                        if kind == FC:
                            tasks.append((at, n, relu, (b, k, bank)))
                        if kind == Y:
                            tasks.append((at, n, spikes, (b, k)))
                            tasks.append((min(at + 4, STEPS), n, gate, (b, k)))
                        if kind == PROJ:
                            tasks.append((at, n, combine, (b, k, bank)))
                        if kind == Q:
                            tasks.append((at, n, q_split, (b + 1, k, bank)))
                        if kind == C:
                            tasks.append((at, n, c_rows, (b + 1, k, bank)))
                    if prep:
                        for t in range(TT):
                            tasks.append((12 + t, -1, ln_stats, (b + 1, t)))
                            tasks.append((24 + t, -1, ln_apply, (b + 1, t)))
                    if not prep and not exact:
                        tasks.append((STEPS // 4, -1, set_flag, ()))
                    for unit in range(UNITS):
                        tasks.append((TT * (unit + 1), 100, normalise, (b, unit)))
                    for n, (kind, k) in enumerate(TAIL):
                        tasks.append((STEPS + 1, 100, combine, (b, k, aux[(len(order) + n) % 2])))
                    for _, _, task, args in sorted(tasks, key=lambda task: (task[0], task[1])):
                        task(*args)

                batches(dve, body, exact)

            run(bounded, False)
            in_general(dve, run)

        @block.gpsimd
        def _(pool):
            def run(s, exact):
                def inv_std(b):
                    wait(pool, s.xn_set, b * 8)
                    wait_apart(pool, s.aggr_set, b * 8 + 8)
                    nc.gpsimd.tensor_scalar(var_eps[:, :], mean_var[:, :, 1], LN_EPS, None, ALU.add).then_inc(s.veps_set, 1)
                    pool.wait_ge(s.veps_set, b + 1)
                    nc.gpsimd.tensor_tensor(rstd[:, :], var_eps[:, :], minus_half[:, :], ALU.pow).then_inc(s.rstd_set, 1)

                def square_q(b, k):
                    chunk, half = k % 2, k // 2
                    cols = slice(half * HALF, (half + 1) * HALF)
                    pool.wait_ge(s.qhi_set, b * 4 + (k + 1))
                    wait(pool, s.pe_done[C], b * 2)
                    nc.gpsimd.tensor_tensor(q_sq[:, chunk, cols], q_hi[:, chunk, cols], q_hi[:, chunk, cols], ALU.mult).then_inc(s.sq_set, 1)

                def place_v(b, g):
                    wait(pool, s.pv_done, (b - 1) * 64 + (NG + g + 1) * TT)
                    wait_apart(pool, s.v_staged, b * 4 + 4)
                    at = 16 * (g % 2)
                    nc.gpsimd.tensor_copy(v_ones[:, :, G * g:G * g + G, at:at + DH],
                                          v_stage[:, :, G * g * DH:(G * g + G) * DH].rearrange("p t (h e) -> p t h e", h=G)).then_inc(s.vones_set, 1)

                def square_h(b, k):
                    f = k % KF
                    pool.wait_ge(s.relu_set, b * 16 + (k + 1))
                    wait(pool, s.pe_done[Y], b * 4 + (2 * (k // KF)))
                    nc.gpsimd.tensor_tensor(h_t[:, f, :], r[:, k % 2, :], r[:, k % 2, :], ALU.mult).then_inc(s.h_set, 1)

                pool.wait_ge(w_set, 2)
                inv_std(0)
                if not exact:
                    for k in range(4):
                        square_q(0, k)
                pool.wait_ge(v_set, 1)
                for g in range(NG):
                    place_v(0, g)

                def body(b, prep):
                    _, done = schedule(prep)
                    tasks = [(done[(FC, k)], square_h, (b, k)) for k in range(COUNT[FC])]
                    if prep:
                        tasks.append((20, inv_std, (b + 1,)))
                        if not exact:
                            tasks += [(done[(Q, k)], square_q, (b + 1, k)) for k in range(COUNT[Q])]
                        tasks += [(max(done[(V, 3)] + 1, TT * (NG + g + 1)), place_v, (b + 1, g)) for g in range(NG)]
                    for _, task, args in sorted(tasks, key=lambda task: task[0]):
                        task(*args)

                batches(pool, body, exact)

            run(bounded, False)
            in_general(pool, run)


def kernel(L0_attn_x, L0_attn_Wq, L0_attn_Wp, L0_attn_bp, L0_ffn_W_fc, L0_ffn_W_proj):
    import numpy as np
    import concourse.bacc as bacc
    from concourse.bass_utils import run_bass_kernel_spmd

    x, wq, wp, bp, wfc, wproj = (np.asarray(a) for a in (L0_attn_x, L0_attn_Wq, L0_attn_Wp, L0_attn_bp, L0_ffn_W_fc, L0_ffn_W_proj))
    wp_rows = wp.T.reshape(NG // 2, 2, G, DH, D)
    wp_s = wp_rows.transpose(2, 1, 3, 0, 4).reshape(P, NG // 2, D)
    ident = np.eye(P, dtype=np.float32)
    p = np.arange(P)
    strip = np.stack([(p % 32 < 16), (p % 32 >= 16)], 1).astype(np.float32)
    head_sum = np.zeros((P, KD, H), np.float32)
    for k in range(KD):
        head_sum[p, k, 8 * k + p // DH] = 1.0
    arrays = {
        "x": x, "wq_t": wq.transpose(0, 2, 1), "wp_s": wp_s, "bp": bp,
        "wfc_t": wfc.T.reshape(KD, P, F).transpose(1, 0, 2),
        "wproj_t": wproj.T.reshape(KF, P, D).transpose(1, 0, 2),
        "consts": np.concatenate([ident, strip, head_sum.reshape(P, -1)], 1),
    }
    arrays = {k: np.ascontiguousarray(v) for k, v in arrays.items()}
    nc = bacc.Bacc("TRN2", target_bir_lowering=False, num_devices=1)
    args = {k: nc.dram_tensor(k, v.shape, FP32, kind="ExternalInput").ap() for k, v in arrays.items()}
    q_scratch = nc.dram_tensor("q_scratch", (H, 2, DH, N), FP16, kind="Internal").ap()
    c_scratch = nc.dram_tensor("c_scratch", (H, N), FP16, kind="Internal").ap()
    q_own_scratch = nc.dram_tensor("q_own_scratch", (H, DH, N), FP32, kind="Internal").ap()
    max_scratch = nc.dram_tensor("max_scratch", (P, P), FP32, kind="Internal").ap()
    bound_scratch = nc.dram_tensor("bound_scratch", (H, 1), FP32, kind="Internal").ap()
    out = nc.dram_tensor("out", (B, N, D), FP32, kind="ExternalOutput").ap()
    build(nc, **args, q_scratch=q_scratch, c_scratch=c_scratch, q_own_scratch=q_own_scratch,
          max_scratch=max_scratch, bound_scratch=bound_scratch, out=out)
    got = run_bass_kernel_spmd(nc, [arrays], core_ids=[0])
    return got.results[0]["out"]
```

```python
from contextlib import ExitStack

import concourse.bass as bass
from concourse import mybir

FP32 = mybir.dt.float32
FP16 = mybir.dt.float16
BF16 = mybir.dt.bfloat16
INT32 = mybir.dt.int32
ALU = mybir.AluOpType
ACT = mybir.ActivationFunctionType
AX = mybir.AxisListType

B, N, D = 16, 1024, 256
H, DH = 16, 16
F = 4 * D
P = 128
TT = N // P
KD = D // P
KF = F // P
HALF = 512
NH = N // HALF
G = 4
NG = H // G
UNITS = NH * NG
STEPS = UNITS * TT
STRIP = P // G
LN_EPS = 1e-5
BETA, THRESHOLD, SPIKE_STEPS = 0.9, 1.0, 5

QS = 1024.0
SCORE_SCALE = 4.0 / (QS * QS)
CROW = 4096.0
SHIFT = 15.5
R2MAX = 130.0

XS = 1024.0
WS = 4096.0
HS = 64.0
WMAX = 15.0
W2MAX = 3.5


def spike_thresholds():
    import numpy as np

    def count(y):
        mem, spikes = np.float32(0), 0
        for _ in range(SPIKE_STEPS):
            reset = np.float32(mem - np.float32(THRESHOLD) > 0)
            mem = np.float32(np.float32(np.float32(BETA) * mem) + y) - reset * np.float32(THRESHOLD)
            spikes += int(mem - np.float32(THRESHOLD) > 0)
        return spikes

    found = []
    for k in range(1, SPIKE_STEPS + 1):
        low, high = 0, int(np.float32(64.0).view(np.int32))
        while high - low > 1:
            mid = (low + high) // 2
            low, high = (low, mid) if count(np.int32(mid).view(np.float32)) >= k else (mid, high)
        found.append(float(np.int32(high).view(np.float32)))
    return found


FC, Y, PROJ, XT, Q, C, V = "fc", "y", "proj", "xt", "q", "c", "v"
COST = {FC: 1.35, Y: 5.3, PROJ: 1.8, XT: 0.35, Q: 0.7, C: 0.45, V: 0.75}
COUNT = {FC: KF * NH, Y: TT // 2, PROJ: TT // 2, XT: KD * NH, Q: KD * NH, C: NH, V: TT // 2}
PREP = [(XT, k) for k in range(4)] + [(Q, k) for k in range(4)] + [(C, k) for k in range(2)] \
    + [(V, k) for k in range(4)]
TAIL = [(PROJ, k) for k in range(2, 4)]
PARTS = {FC: 2, Y: 16, PROJ: 4, XT: 1, Q: 1, C: 1, V: 1}


def prep_groups(exact):
    return [group for group in PREP if not (exact and group[0] == C)]


def batch_groups(first, last, exact):
    own = [(0, FC, k) for k in range(8)] + [(0, Y, k) for k in range(2)] + [(0, FC, k) for k in range(8, 16)] \
        + [(0, PROJ, k) for k in range(2)]
    tail = [] if first else [(-1, kind, k) for kind, k in TAIL]
    prep = [] if last else [(1, kind, k) for kind, k in prep_groups(exact)]
    return own[:3] + tail + own[3:] + prep + [(0, Y, k) for k in range(2, 4)]


def schedule(groups):
    total = sum(COST[kind] for _, kind, _ in groups)
    at, step, out, done = 0.0, 0, [[] for _ in range(STEPS)], []
    for n, (offset, kind, k) in enumerate(groups):
        for part in range(PARTS[kind]):
            step = max(step, int(at / total * STEPS))
            if kind == PROJ:
                step = max(step, STEPS // 2 + 3 if offset == 0 else 3)
            step = min(step, STEPS - 1)
            out[step].append((kind, k, part, n))
            at += COST[kind] / PARTS[kind]
        done.append(step)
    return out, done


class Signals:

    def __init__(self, sem, way):
        self.x_in = sem(f"{way}_x_in")
        self.x_again = sem(f"{way}_x_again")
        self.out_done = sem(f"{way}_out_done")
        self.q_out = sem(f"{way}_q_out")
        self.c_out = sem(f"{way}_c_out")
        self.scored = sem(f"{way}_scored")
        self.pv_done = sem(f"{way}_pv_done")
        self.exp_done = sem(f"{way}_exp_done")
        self.xhi_set = sem(f"{way}_xhi_set")
        self.xnt_set = sem(f"{way}_xnt_set")
        self.v_staged = sem(f"{way}_v_staged")
        self.y_set = sem(f"{way}_y_set")
        self.th_set = sem(f"{way}_th_set")
        self.stat_set = sem(f"{way}_stat_set")
        self.aggr_set = sem(f"{way}_aggr_set")
        self.xn_set = sem(f"{way}_xn_set")
        self.relu_set = sem(f"{way}_relu_set")
        self.hhi_set = sem(f"{way}_hhi_set")
        self.fc_taken = self.hhi_set if way == "bounded" else self.relu_set
        self.qhi_set = sem(f"{way}_qhi_set")
        self.qlo_set = sem(f"{way}_qlo_set")
        self.c_set = sem(f"{way}_c_set")
        self.min_set = sem(f"{way}_min_set")
        self.cnt_link = sem(f"{way}_cnt_link")
        self.gate_set = sem(f"{way}_gate_set")
        self.acct_set = sem(f"{way}_acct_set")
        self.recip_set = sem(f"{way}_recip_set")
        self.scaled_set = sem(f"{way}_scaled_set")
        self.res_set = sem(f"{way}_res_set")
        self.s_set = sem(f"{way}_s_set")
        self.comb_link = sem(f"{way}_comb_link")
        self.comb_set = sem(f"{way}_comb_set")
        self.veps_set = sem(f"{way}_veps_set")
        self.rstd_set = sem(f"{way}_rstd_set")
        self.rsq_set = sem(f"{way}_rsq_set")
        self.h_set = sem(f"{way}_h_set")
        self.sq_set = sem(f"{way}_sq_set")
        self.vones_set = sem(f"{way}_vones_set")
        self.max_scored = sem(f"{way}_max_scored")
        self.max_set = sem(f"{way}_max_set")
        self.max_t = sem(f"{way}_max_t")
        self.max_out = sem(f"{way}_max_out")
        self.max_in = sem(f"{way}_max_in")
        self.stack_in = [sem(f"{way}_stack_in{g}") for g in range(NG)]
        self.pe_done = {kind: sem(f"{way}_pe_{kind}") for kind in COUNT}


def build(nc, x, wq_t, wp_s, bp, wfc_t, wproj_t, consts, q_scratch, c_scratch, q_own_scratch,
          max_scratch, bound_scratch, out):
    thresholds = spike_thresholds()
    x_v = x.rearrange("b (p t) d -> b p t d", p=P)
    out_v = out.rearrange("b (p t) d -> b p t d", p=P)

    ctx = ExitStack()
    with ctx:
        def sb(name, shape, dtype):
            return ctx.enter_context(nc.sbuf_tensor(name, shape, dtype))

        def sem(name):
            return ctx.enter_context(nc.semaphore(name))

        w_fc = sb("w_fc", [P, KD, F], FP32)
        w_proj = sb("w_proj", [P, KF, D], FP32)
        w_p = sb("w_p", [P, NG // 2, D], FP32)
        w_q = sb("w_q", [P, KD, P], FP32)
        w_q16 = sb("w_q16", [P, 2, KD, P], FP16)
        b_p = sb("b_p", [P, D], FP32)
        const = sb("const", [P, P + KD * H + 1], FP32)
        ident = const[:, 0:P]
        ones_column = const[:, P + KD * H:]
        head_sum = sb("head_sum", [P, KD, H], BF16)
        minus_half = sb("minus_half", [P, TT], FP32)
        x_tok = sb("x_tok", [P, TT, D], FP32)
        stats = sb("stats", [P, TT, 6], FP32)
        mean_var = sb("mean_var", [P, TT, 2], FP32)
        var_eps = sb("var_eps", [P, TT], FP32)
        rstd = sb("rstd", [P, TT], FP32)
        xn_t = sb("xn_t", [P, KD, N], FP32)
        q_hi = sb("q_hi", [P, KD, N], FP16)
        q_lo = sb("q_lo", [P, KD, N], FP16)
        q_sq = sb("q_sq", [P, KD, N], BF16)
        key_stack = sb("key_stack", [96 + H, H, N], FP16)
        c_row = key_stack[96:96 + H, 0, :]
        query_stack = sb("query_stack", [65, H, N], FP16)
        v_stage = sb("v_stage", [P, TT, D], FP32)
        v_ones = sb("v_ones", [P, TT, H, STRIP], FP32)
        NE = 4
        e = sb("e", [P, NE, 2, HALF], FP32)
        acc_t = sb("acc_t", [P, HALF // STRIP, STRIP], FP32)
        recip = sb("recip", [P, HALF // STRIP, 1], FP32)
        scaled_t = sb("scaled_t", [P, HALF // STRIP, STRIP], FP32)
        res = sb("res", [P, NH, NG // 2, HALF], FP32)
        r = sb("r", [P, 2, HALF], FP32)
        r_squared = sb("r_squared", [P, HALF], FP32)
        h_t = sb("h_t", [P, KF, HALF], FP32)
        y_sb = sb("y_sb", [P, 2, HALF], FP32)

        def halves(tensor):
            flat = tensor[:, :, :].rearrange("p a b -> p (a b)").bitcast(FP16)
            return flat.rearrange("p (s a b) -> p s a b", s=2, a=tensor.shape[1])

        w_fc16, w_proj16, xn_t16, h_t16 = (halves(t) for t in (w_fc, w_proj, xn_t, h_t))
        cnt = sb("cnt", [P, TT // 2, HALF], FP32)
        x_out = sb("x_out", [P, TT // NH, D], FP32)
        s_b = sb("s_b", [P, HALF], FP32)
        c_min = sb("c_min", [H, 2], FP32)
        used = sb("used", [P, 4], FP32)
        used_most = sb("used_most", [P, 1], FP32)
        flag = sb("flag", [1, 1], INT32)
        used_all = x_tok[0:1, 0, 0:P]
        q_own = x_tok[:, :, :].rearrange("p t d -> p (t d)").rearrange("p (k n) -> p k n", k=KD)
        q_rows = [stack[0:65, :, :].bitcast(FP32) for stack in (key_stack, query_stack)]
        pick_max = q_hi[0:33, 0, 0:2 * P].bitcast(FP32)
        row_max = q_sq[:, 0, 0:2 * H * TT].bitcast(FP32).rearrange("p (h t) -> p h t", h=H)
        row_max_t = q_sq[:, 1, 0:2 * P].bitcast(FP32)

        scores = [ctx.enter_context(nc.psum_tensor(f"scores{i}", [P, 2, HALF], FP32)) for i in range(2)]
        acc = [ctx.enter_context(nc.psum_tensor(f"acc{i}", [P, HALF], FP32)) for i in range(2)]
        aux = [ctx.enter_context(nc.psum_tensor(f"aux{i}", [P, HALF], FP32)) for i in range(2)]

        fc_stage = e[:, 0:2, :, :].rearrange("p a b n -> p (a b n)").rearrange("p (k f) -> p k f", k=KD)
        proj_stage = e[:, 2:4, :, :].rearrange("p a b n -> p (a b n)").rearrange("p (k f) -> p k f", k=KF)
        fc_squares = h_t[:, 0:4, :].rearrange("p a b -> p (a b)").rearrange("p (k f) -> p k f", k=KD)
        proj_squares = h_t[:, 4:8, :].rearrange("p a b -> p (a b)").rearrange("p (k f) -> p k f", k=KF)

        wq_squares = r[:, 0, 0:KD * P].rearrange("p (k f) -> p k f", k=KD)

        w_in, wq_in, w_set, v_set = sem("w_in"), sem("wq_in"), sem("w_set"), sem("v_set")
        staged, wq_split, w_split, w_again = sem("staged"), sem("wq_split"), sem("w_split"), sem("w_again")
        square_link, squared, norms, used_set = sem("square_link"), sem("squared"), sem("norms"), sem("used_set")
        c_init, const_in = sem("c_init"), sem("const_in")
        flag_part, flag_out, flag_in, flag_set = sem("flag_part"), sem("flag_out"), sem("flag_in"), sem("flag_set")
        cleared = sem("cleared")
        bounded, general = Signals(sem, "bounded"), Signals(sem, "general")

        def wait(eng, semaphore, value):
            if not (isinstance(value, int) and value <= 0):
                eng.wait_ge(semaphore, value)

        def wait_apart(eng, semaphore, value):
            wait(eng, semaphore, value)
            eng.nop(nofuse=True)

        def emptied(s, kind, b, k):
            return {FC: (s.fc_taken, b * 16 + (k + 1)), Y: (s.y_set, b * 4 + (k + 1)), PROJ: (s.s_set, b * 4 + (k + 1)),
                    XT: (s.xnt_set, b * 4 + (k + 1)), Q: (s.qlo_set, b * 4 + (k + 1)), C: (s.c_set, b * 2 + (k + 1)),
                    V: (s.v_staged, b * 4 + (k + 1))}[kind]

        block = ctx.enter_context(nc.Block())

        def batches(eng, body):
            body(0, True, False)
            with eng.Fori(1, B - 1) as b:
                body(b, False, False)
            body(B - 1, False, True)

        def in_general(eng, run):
            eng.wait_ge(bounded.out_done, B * 32)
            eng.wait_ge(flag_set, 1)
            beyond = eng.value_load(flag[0:1, 0:1], min_val=0, max_val=1)
            with eng.If(beyond > 0):
                run(general, True)

        @block.sync
        def _(sp):
            sp.dma_start(x_tok[:, :, :], x_v[0, :, :, :]).then_inc(bounded.x_in, 16)
            sp.dma_start(const[:, :], consts).then_inc(const_in, 16)
            sp.wait_ge(w_set, 1)
            for h in range(H):
                p = DH * h % P
                sp.dma_start(w_q[p:p + DH, h // 8, p:p + DH], wq_t[h, :, :]).then_inc(wq_in, 16)
            for dst, src in ((fc_stage, wfc_t), (proj_stage, wproj_t)):
                sp.dma_start(dst, src).then_inc(staged, 16)
            for dst, src in ((w_p[:, :, :], wp_s), (b_p[:, :], bp.rearrange("(a d) -> a d", a=1).broadcast_to((P, D)))):
                sp.dma_start(dst, src).then_inc(w_in, 16)

            def run(s, exact):
                stack_loads = 16 * (2 if exact else 7)

                def load_x(b):
                    wait_apart(sp, s.pe_done[XT], b * 4)
                    if exact:
                        wait(sp, s.q_out, b * 32)
                    sp.dma_start(x_tok[:, :, :], x_v[b, :, :, :]).then_inc(s.x_in, 16)

                def store_q(b):
                    wait_apart(sp, s.qlo_set, b * 4 + 4)
                    for g in range(NG):
                        wait_apart(sp, s.stack_in[g], b * stack_loads)
                    if exact:
                        for k in range(KD):
                            sp.dma_start(q_own_scratch[8 * k:8 * k + 8, :, :], q_own[:, k, :]).then_inc(s.q_out, 16)
                        wait_apart(sp, s.q_out, b * 32 + 32)
                        return
                    for part, q in enumerate((q_hi, q_lo)):
                        for k in range(KD):
                            sp.dma_start(q_scratch[8 * k:8 * k + 8, part, :, :], q[:, k, :]).then_inc(s.q_out, 16)
                    sp.wait_ge(s.c_set, b * 2 + 2)
                    sp.dma_start(c_scratch, c_row).then_inc(s.c_out, 16)
                    wait_apart(sp, s.q_out, b * 64 + 64)
                    wait_apart(sp, s.c_out, b * 16 + 16)

                def load_stack(b, g):
                    wait_apart(sp, s.scored, (b - 1) * 128 + (NG + g + 1) * 16)
                    heads = slice(G * g, G * g + G)
                    if exact:
                        for half in range(NH):
                            sp.dma_start(q_rows[half][0:DH, heads, :],
                                         q_own_scratch[heads, :, half * HALF:(half + 1) * HALF].rearrange("h e n -> e h n")) \
                                .then_inc(s.stack_in[g], 16)
                        return
                    for rep in range(2):
                        sp.dma_start(query_stack[32 * rep:32 * rep + 32, heads, :],
                                     q_scratch[heads, :, :, :].rearrange("h s e n -> (s e) h n")).then_inc(s.stack_in[g], 16)
                        for part in range(2):
                            row = 32 * part + 16 * rep
                            sp.dma_start(key_stack[row:row + 16, heads, :],
                                         q_scratch[heads, part, :, :].rearrange("h e n -> e h n")).then_inc(s.stack_in[g], 16)
                    sp.dma_start(query_stack[64:65, heads, :],
                                 c_scratch[heads, :].rearrange("(a h) n -> a h n", a=1)).then_inc(s.stack_in[g], 16)

                def store_out(b, half):
                    sp.wait_ge(s.comb_set, b * 4 + (2 * half + 2))
                    sp.dma_start(out_v[b, :, 4 * half:4 * half + 4, :], x_out[:, :, :]).then_inc(s.out_done, 16)

                def load_again(b, half):
                    wait(sp, s.out_done, b * 32 + 16 * half)
                    sp.dma_start(x_out[:, :, :], x_v[b, :, 4 * half:4 * half + 4, :]).then_inc(s.x_again, 16)

                def place_max(b):
                    sp.wait_ge(s.max_set, b * 129 + 129)
                    sp.dma_start(max_scratch, row_max_t).then_inc(s.max_out, 16)
                    wait_apart(sp, s.max_out, b * 16 + 16)
                    wait(sp, s.scored, b * 128)
                    for half in range(NH):
                        sp.dma_start(q_rows[half][32:33, :, :],
                                     max_scratch.rearrange("(a h s t) n -> s a h (t n)", a=1, h=H, s=NH)[half]).then_inc(s.max_in, 16)

                def collect_bound():
                    sp.wait_ge(used_set, 6)
                    sp.dma_start(bound_scratch, used_most[:, :]).then_inc(flag_out, 16)
                    sp.wait_ge(flag_out, 16)
                    sp.wait_ge(s.pe_done[XT], B * 4)
                    sp.dma_start(used_all, bound_scratch.rearrange("p a -> a p")).then_inc(flag_in, 16)

                if exact:
                    load_x(0)
                    for dst, src in ((w_fc[:, :, :], wfc_t), (w_proj[:, :, :], wproj_t)):
                        sp.dma_start(dst, src).then_inc(w_again, 16)
                store_q(0)
                if exact:
                    sp.wait_ge(cleared, 4)
                for g in range(NG):
                    load_stack(0, g)

                def body(b, first, last):
                    if exact:
                        place_max(b)
                    elif last:
                        collect_bound()
                    if not last:
                        load_x(b + 1)
                    if not first:
                        store_out(b - 1, 1)
                    load_again(b, 0)
                    store_out(b, 0)
                    load_again(b, 1)
                    if not last:
                        store_q(b + 1)
                        for g in range(NG):
                            load_stack(b + 1, g)

                batches(sp, body)
                store_out(B - 1, 1)
                sp.wait_ge(s.out_done, B * 32)

            run(bounded, False)
            in_general(sp, run)

        @block.tensor
        def _(pe):
            def run(s, exact):
                def product(out, a, b, first=True, last=True):
                    for n, (x, y) in enumerate(((0, 0), (0, 1), (1, 0))):
                        ins = nc.tensor.matmul(out, a(x), b(y), start=first and n == 0, stop=last and n == 2)
                    return ins

                def paired(b, kind, k, part, bank):
                    half = k // KF if kind == FC else k // 2
                    cols = slice(half * HALF, (half + 1) * HALF)
                    if kind == FC:
                        f = k % KF
                        return product(bank[:, :], lambda x: w_fc16[:, x, part, f * P:(f + 1) * P],
                                       lambda x: xn_t16[:, x, part, cols], part == 0, part == 1)
                    if kind == Y:
                        t, f = part // KF, part % KF
                        if part < KF:
                            pe.wait_ge(s.h_set, b * 16 + (8 * half + f + 1))
                        col = (2 * k + t) % 4 * P
                        return product(bank[:, t * D:(t + 1) * D], lambda x: h_t16[:, x, f, col:col + P],
                                       lambda x: w_proj16[:, x, f, :], f == 0, f == KF - 1)
                    if kind == Q:
                        chunk = k % 2
                        pe.wait_ge(s.xnt_set, b * 4 + 4)
                        return product(bank[:, :], lambda x: w_q16[:, x, chunk, :], lambda x: xn_t16[:, x, chunk, cols])
                    for t in range(2):
                        for chunk in range(KD):
                            tokens = slice((2 * k + t) * P, (2 * k + t + 1) * P)
                            ins = product(bank[:, t * D + chunk * P:t * D + (chunk + 1) * P],
                                          lambda x: xn_t16[:, x, chunk, tokens], lambda x: w_q16[:, x, chunk, :])
                    return ins

                def aux_part(b, piece, before):
                    kind, k, part, n = piece
                    bank = aux[n % 2]
                    if part == 0:
                        wait(pe, *before)
                    if not exact and kind in (FC, Y, Q, V):
                        ins = paired(b, kind, k, part, bank)
                    elif kind == FC:
                        half, f = k // KF, k % KF
                        ins = nc.tensor.matmul(bank[:, :], w_fc[:, part, f * P:(f + 1) * P],
                                               xn_t[:, part, half * HALF:(half + 1) * HALF], start=part == 0, stop=part == 1)
                    elif kind == Y:
                        t, f = part // KF, part % KF
                        if part < KF:
                            pe.wait_ge(s.h_set, b * 16 + (8 * (k // 2) + f + 1))
                        col = (2 * k + t) % 4 * P
                        ins = nc.tensor.matmul(bank[:, t * D:(t + 1) * D], h_t[:, f, col:col + P], w_proj[:, f, :],
                                               start=f == 0, stop=f == KF - 1)
                    elif kind == PROJ:
                        t, pair = part // 2, part % 2
                        half = k // 2
                        if part == 0:
                            pe.wait_ge(s.res_set, b * 4 + (2 * half + 2))
                        col = (2 * k + t) % 4 * P
                        ins = nc.tensor.matmul(bank[:, t * D:(t + 1) * D], res[:, half, pair, col:col + P], w_p[:, pair, :],
                                               start=pair == 0, stop=pair == 1)
                    elif kind == XT:
                        chunk, half = k % 2, k // 2
                        pe.wait_ge(s.xn_set, b * 8 + (4 * half + 4))
                        for t in range(4):
                            ins = nc.tensor.transpose(bank[:, t * P:(t + 1) * P],
                                                      x_tok[:, 4 * half + t, chunk * P:(chunk + 1) * P], ident)
                    elif kind == Q:
                        chunk, half = k % 2, k // 2
                        pe.wait_ge(s.xnt_set, b * 4 + 4)
                        ins = nc.tensor.matmul(bank[:, :], w_q[:, chunk, :], xn_t[:, chunk, half * HALF:(half + 1) * HALF],
                                               start=True, stop=True)
                    elif kind == C:
                        pe.wait_ge(s.sq_set, b * 4 + (2 * k + 2))
                        for chunk in range(KD):
                            ins = nc.tensor.matmul(bank[0:H, :], head_sum[:, chunk, :], q_sq[:, chunk, k * HALF:(k + 1) * HALF],
                                                   start=chunk == 0, stop=chunk == KD - 1)
                    else:
                        for t in range(2):
                            for chunk in range(KD):
                                ins = nc.tensor.matmul(bank[:, t * D + chunk * P:t * D + (chunk + 1) * P],
                                                       xn_t[:, chunk, (2 * k + t) * P:(2 * k + t + 1) * P],
                                                       w_q[:, chunk, :], start=True, stop=True)
                    if part == PARTS[kind] - 1:
                        ins.then_inc(s.pe_done[kind], 1)

                def pv(b, i):
                    unit, j = i // TT, i % TT
                    half, g = unit // NG, unit % NG
                    if j == 0:
                        wait(pe, s.acct_set, b * 8 + (unit - 1))
                        if half == 0:
                            pe.wait_ge(s.vones_set, b * 4 + (g + 1))
                    pe.wait_ge(s.exp_done, b * 128 + (2 * i + 2))
                    for n in range(G):
                        tile = (2 * i + n // 2) % NE
                        ins = nc.tensor.matmul(acc[unit % 2][STRIP * n:STRIP * (n + 1), :], v_ones[:, j, G * g + n, :],
                                               e[:, tile, n % 2, :], start=j == 0, stop=j == TT - 1)
                    ins.then_inc(s.pv_done, 1)

                def row_maxima(b):
                    for g in range(NG):
                        pe.wait_ge(s.stack_in[g], b * 32 + 32)
                    for i in range(H * TT):
                        head, t = i // TT, i % TT
                        if i >= 2:
                            pe.wait_ge(s.max_set, b * 129 + (i - 1))
                        for half in range(NH):
                            ins = nc.tensor.matmul(scores[i % 2][:, half, :],
                                                   q_rows[t // 4][0:DH, head, t % 4 * P:(t % 4 + 1) * P],
                                                   q_rows[half][0:DH, head, :], start=True, stop=True)
                        ins.then_inc(s.max_scored, 1)
                    pe.wait_ge(s.max_set, b * 129 + 128)
                    nc.tensor.transpose(scores[0][:, 0, 0:P], row_max[:, :, :].rearrange("p h t -> p (h t)"), ident) \
                        .then_inc(s.max_t, 1)
                    pe.wait_ge(s.max_in, b * 32 + 32)

                def score(bank, head, half, j):
                    if not exact:
                        return nc.tensor.matmul(bank, key_stack[0:65, head, j * P:(j + 1) * P],
                                                query_stack[:, head, half * HALF:(half + 1) * HALF], start=True, stop=True)
                    nc.tensor.matmul(bank, q_rows[j // 4][0:DH, head, j % 4 * P:(j % 4 + 1) * P],
                                     q_rows[half][0:DH, head, :], start=True, stop=False)
                    return nc.tensor.matmul(bank, pick_max, q_rows[half][0:33, head, :], start=False, stop=True)

                pe.wait_ge(const_in, 16)
                pe.wait_ge(wq_split, 2)
                pe.wait_ge(w_set, 3)
                for n, (kind, k) in enumerate(prep_groups(exact)):
                    before = emptied(s, prep_groups(exact)[n - 2][0], 0, prep_groups(exact)[n - 2][1]) if n >= 2 else (w_in, 0)
                    aux_part(0, (kind, k, 0, n), before)
                pe.wait_ge(v_set, 2)
                pe.wait_ge(w_in, 2 * 16)
                if exact:
                    pe.wait_ge(cleared, 4)
                    pe.wait_ge(w_again, 32)
                else:
                    pe.wait_ge(squared, 1)
                    for half in range(2):
                        for chunk in range(KD):
                            ins = nc.tensor.matmul(scores[0][0:1, half, :], ones_column, fc_squares[:, chunk, half * HALF:(half + 1) * HALF],
                                                   start=chunk == 0, stop=chunk == KD - 1)
                    ins.then_inc(norms, 1)
                    pe.wait_ge(w_split, 4)
                    pe.wait_ge(used_set, 3)

                def body(b, first, last):
                    groups = batch_groups(first, last, exact)
                    steps, _ = schedule(groups)
                    order = ([(0, V, 2), (0, V, 3)] if first else [(b - 1, Y, 2), (b - 1, Y, 3)]) \
                        + [(b + offset, kind, k) for offset, kind, k in groups]
                    if exact:
                        wait(pe, s.exp_done, b * 128)
                        row_maxima(b)
                    for i in range(STEPS):
                        unit, j = i // TT, i % TT
                        half, g = unit // NG, unit % NG
                        if j == 0 and half == 0 and not exact:
                            pe.wait_ge(s.stack_in[g], b * 112 + 112)
                        for pair in range(2):
                            tile = 2 * i + pair
                            wait(pe, s.exp_done, b * 128 + (tile - 1))
                            for n in range(2):
                                head = G * g + 2 * pair + n
                                ins = score(scores[tile % 2][:, n, :], head, half, j)
                            ins.then_inc(s.scored, 1)
                        if i:
                            pv(b, i - 1)
                        elif not first:
                            pv(b - 1, STEPS - 1)
                        for piece in steps[i]:
                            n = piece[3]
                            aux_part(order[n + 2][0], piece, emptied(s, order[n][1], order[n][0], order[n][2]))

                batches(pe, body)
                pv(B - 1, STEPS - 1)
                for n, (kind, k) in enumerate(TAIL):
                    for part in range(PARTS[kind]):
                        aux_part(B - 1, (kind, k, part, n), emptied(s, Y, B - 1, 2 + n))

            run(bounded, False)
            in_general(pe, run)

        @block.scalar
        def _(act):
            def run(s, exact):
                def evac(b, kind, k, bank):
                    if kind == XT:
                        chunk, half = k % 2, k // 2
                        wait(act, s.pe_done[FC], b * 16)
                        wait(act, s.pe_done[V], b * 4)
                        act.wait_ge(s.pe_done[XT], b * 4 + (k + 1))
                        if not exact:
                            nc.scalar.activation(xn_t16[:, 0, chunk, half * HALF:(half + 1) * HALF], bank[:, :], ACT.Copy,
                                                 scale=XS).then_inc(s.xhi_set, 1)
                            return
                        nc.scalar.activation(xn_t[:, chunk, half * HALF:(half + 1) * HALF], bank[:, :], ACT.Copy).then_inc(s.xnt_set, 1)
                    elif kind == V:
                        wait(act, s.vones_set, b * 4)
                        act.wait_ge(s.pe_done[V], b * 4 + (k + 1))
                        nc.scalar.activation(v_stage[:, 2 * k:2 * k + 2, :], bank[:, :].rearrange("p (t d) -> p t d", t=2),
                                             ACT.Copy, scale=1.0 if exact else 1.0 / (XS * WS)).then_inc(s.v_staged, 1)
                    elif kind == Y:
                        wait(act, s.gate_set, b * 4 + (k - 1))
                        act.wait_ge(s.pe_done[Y], b * 4 + (k + 1))
                        nc.scalar.activation(y_sb[:, k % 2, :], bank[:, :], ACT.Copy, scale=1.0 if exact else 1.0 / (HS * WS)).then_inc(s.y_set, 1)

                def tanh(b, k):
                    act.wait_ge(s.cnt_link, b * 20 + (k + 1) * 5)
                    nc.scalar.activation(y_sb[:, k % 2, :], cnt[:, k, :], ACT.Tanh, scale=0.5 / SPIKE_STEPS).then_inc(s.th_set, 1)

                if not exact:
                    act.wait_ge(wq_in, H * 16)
                    nc.scalar.activation(w_q16[:, 0, :, :], w_q[:, :, :], ACT.Copy, scale=WS).then_inc(wq_split, 1)
                for n, (kind, k) in enumerate(prep_groups(exact)):
                    if kind in (XT, V):
                        evac(0, kind, k, aux[n % 2])

                if not exact:
                    act.wait_ge(staged, 32)
                    nc.scalar.activation(w_fc16[:, 0, :, :], fc_stage, ACT.Copy, scale=WS).then_inc(w_split, 1)
                    nc.scalar.activation(w_proj16[:, 0, :, :], proj_stage, ACT.Copy, scale=WS).then_inc(w_split, 1)
                    act.wait_ge(w_split, 4)
                    act.wait_ge(squared, 2)
                    act.wait_ge(used_set, 3)

                def body(b, first, last):
                    groups = batch_groups(first, last, exact)
                    _, done = schedule(groups)
                    tasks = []
                    for n, (offset, kind, k) in enumerate(groups):
                        if kind in (XT, V, Y):
                            tasks.append((done[n], n, evac, (b + offset, kind, k, aux[n % 2])))
                        if kind == Y and k < 3:
                            tasks.append((min(done[n] + 4, STEPS), n, tanh, (b, k)))
                    if not first:
                        tasks.append((1, -1, tanh, (b - 1, 3)))
                    tasks.sort(key=lambda task: task[:2])
                    for i in range(STEPS + 1):
                        if i < STEPS:
                            for tile in (2 * i, 2 * i + 1):
                                act.wait_ge(s.scored, b * 128 + (tile + 1))
                                wait(act, s.pv_done, b * 64 + (tile // 2 - NE // 2 + 1))
                                nc.scalar.activation(e[:, tile % NE, :, :], scores[tile % 2][:, :, :], ACT.Exp,
                                                     scale=4.0 if exact else SCORE_SCALE).then_inc(s.exp_done, 1)
                        for at, _, task, args in tasks:
                            if at == i:
                                task(*args)

                batches(act, body)
                tanh(B - 1, 3)

            run(bounded, False)
            in_general(act, run)

        @block.vector
        def _(dve):
            nc.vector.memset(w_q[:, :, :], 0.0).then_inc(w_set, 1)
            nc.vector.memset(minus_half[:, :], -0.5).then_inc(w_set, 1)
            dve.wait_ge(const_in, 16)
            nc.vector.tensor_copy(head_sum[:, :, :], const[:, P:P + KD * H].rearrange("p (k h) -> p k h", k=KD)).then_inc(w_set, 1)
            nc.vector.memset(c_min[:, :], 0.0).then_inc(c_init, 1)
            nc.vector.memset(used[:, :], 0.0).then_inc(used_set, 1)

            def run(s, exact):
                def ln_stats(b, t):
                    if t == 0:
                        dve.wait_ge(s.x_in, b * 16 + 16)
                        wait(dve, s.xn_set, b * 8)
                    nc.vector.bn_stats(stats[:, t, :], x_tok[:, t, :]).then_inc(s.stat_set, 1)
                    if t == TT - 1:
                        wait_apart(dve, s.rstd_set, b)
                        wait_apart(dve, s.stat_set, b * 8 + 8)
                        for u in range(TT):
                            nc.vector.bn_aggr(mean_var[:, u, :], stats[:, u, :]).then_inc(s.aggr_set, 1)

                def ln_apply(b, t):
                    dve.wait_ge(s.rstd_set, b + 1)
                    nc.vector.tensor_scalar(x_tok[:, t, :], x_tok[:, t, :], mean_var[:, t, 0:1], rstd[:, t:t + 1],
                                            ALU.subtract, ALU.mult).then_inc(s.xn_set, 1)

                def q_split(b, k, bank):
                    chunk, half = k % 2, k // 2
                    cols = slice(half * HALF, (half + 1) * HALF)
                    dve.wait_ge(s.pe_done[Q], b * 4 + (k + 1))
                    if exact:
                        nc.vector.tensor_scalar(q_own[:, chunk, cols], bank[:, :], 1.0, None, ALU.mult).then_inc(s.qlo_set, 1)
                        return
                    wait(dve, s.q_out, b * 64)
                    wait(dve, s.sq_set, b * 4)
                    nc.vector.tensor_scalar(q_hi[:, chunk, cols], bank[:, :], QS / (XS * WS), None, ALU.mult).then_inc(s.qhi_set, 1)
                    dve.wait_ge(s.qhi_set, b * 4 + (k + 1))
                    nc.vector.scalar_tensor_tensor(q_lo[:, chunk, cols], bank[:, :], QS / (XS * WS), q_hi[:, chunk, cols],
                                                   ALU.mult, ALU.subtract).then_inc(s.qlo_set, 1)

                def c_rows(b, k, bank):
                    dve.wait_ge(s.pe_done[C], b * 2 + (k + 1))
                    wait(dve, s.c_out, b * 16)
                    wait(dve, s.min_set, b * 2)
                    nc.vector.tensor_scalar(c_row[:, k * HALF:(k + 1) * HALF], bank[0:H, :], -1.0 / CROW,
                                            -SHIFT * QS * QS / CROW, ALU.mult, ALU.add).then_inc(s.c_set, 1)
                    if k == NH - 1:
                        dve.wait_ge(s.c_set, b * 2 + 2)
                        nc.vector.tensor_reduce(c_min[:, 1:2], c_row, AX.X, ALU.min).then_inc(s.min_set, 1)
                        dve.wait_ge(s.min_set, b * 2 + 1)
                        nc.vector.tensor_tensor(c_min[:, 0:1], c_min[:, 0:1], c_min[:, 1:2], ALU.min).then_inc(s.min_set, 1)

                def x_lo(b, k, bank):
                    chunk, half = k % 2, k // 2
                    cols = slice(half * HALF, (half + 1) * HALF)
                    dve.wait_ge(s.xhi_set, b * 4 + (k + 1))
                    nc.vector.scalar_tensor_tensor(xn_t16[:, 1, chunk, cols], bank[:, :], XS, xn_t16[:, 0, chunk, cols],
                                                   ALU.mult, ALU.subtract).then_inc(s.xnt_set, 1)

                def split_weights():
                    for n, (w16, stage) in enumerate(((w_fc16, fc_stage), (w_proj16, proj_stage))):
                        dve.wait_ge(w_split, 2 * n + 1)
                        nc.vector.scalar_tensor_tensor(w16[:, 1, :, :], stage, WS, w16[:, 0, :, :],
                                                       ALU.mult, ALU.subtract).then_inc(w_split, 1)

                def relu(b, k, bank):
                    dve.wait_ge(s.pe_done[FC], b * 16 + (k + 1))
                    wait(dve, s.h_set, b * 16 + (k - 1))
                    nc.vector.tensor_scalar(r[:, k % 2, :], bank[:, :], 0.0, 1.0 if exact else HS ** 0.5 / (XS * WS),
                                            ALU.max, ALU.mult).then_inc(s.relu_set, 1)
                    if exact:
                        return
                    wait(dve, s.pe_done[Y], b * 4 + (2 * (k // KF)))
                    dve.wait_ge(s.relu_set, b * 16 + (k + 1))
                    nc.vector.scalar_tensor_tensor(h_t16[:, 0, k % KF, :], bank[:, :], HS ** 0.5 / (XS * WS), r[:, k % 2, :],
                                                   ALU.mult, ALU.mult).then_inc(s.hhi_set, 1)

                def spikes(b, k):
                    dve.wait_ge(s.y_set, b * 4 + (k + 1))
                    wait(dve, s.comb_link, (b - 1) * 4 + k + 1)
                    link = b * 20 + k * 5
                    nc.vector.tensor_scalar(cnt[:, k, :], y_sb[:, k % 2, :], thresholds[0], None, ALU.is_ge).then_inc(s.cnt_link, 1)
                    for n in range(1, SPIKE_STEPS):
                        dve.wait_ge(s.cnt_link, link + n)
                        nc.vector.scalar_tensor_tensor(cnt[:, k, :], y_sb[:, k % 2, :], thresholds[n], cnt[:, k, :],
                                                       ALU.is_ge, ALU.add).then_inc(s.cnt_link, 1)

                def gate(b, k):
                    dve.wait_ge(s.th_set, b * 4 + (k + 1))
                    nc.vector.scalar_tensor_tensor(cnt[:, k, :], y_sb[:, k % 2, :], 1.0, cnt[:, k, :], ALU.add, ALU.mult).then_inc(s.gate_set, 1)

                def normalise(b, unit):
                    pair, odd = unit // 2, unit % 2
                    own, sums = (slice(DH, STRIP), 0) if odd else (slice(0, DH), DH)
                    wait(dve, s.scaled_set, b * 8 + unit)
                    dve.wait_ge(s.pv_done, b * 64 + (unit + 1) * TT)
                    nc.vector.transpose(acc_t[:, :, :].rearrange("p c r -> p (c r)"), acc[unit % 2][:, :]).then_inc(s.acct_set, 1)
                    dve.wait_ge(s.acct_set, b * 8 + (unit + 1))
                    nc.vector.reciprocal(recip[:, :, :], acc_t[:, :, sums:sums + 1]).then_inc(s.recip_set, 1)
                    if not odd:
                        wait(dve, s.res_set, b * 4 + pair)
                    dve.wait_ge(s.recip_set, b * 8 + (unit + 1))
                    nc.vector.tensor_tensor(scaled_t[:, :, own], acc_t[:, :, own],
                                            recip[:, :, :].broadcast_to((P, HALF // STRIP, DH)), ALU.mult).then_inc(s.scaled_set, 1)
                    if odd:
                        wait(dve, s.pe_done[PROJ], (b - 1) * 4 + (2 * (pair // 2) + 2))
                        dve.wait_ge(s.scaled_set, b * 8 + (unit + 1))
                        nc.vector.transpose(res[:, pair // 2, pair % 2, :],
                                            scaled_t[:, :, :].rearrange("p c r -> p (c r)")).then_inc(s.res_set, 1)

                def combine(b, k, bank):
                    dve.wait_ge(s.pe_done[PROJ], b * 4 + (k + 1))
                    wait(dve, s.comb_set, b * 4 + k)
                    for t in range(2):
                        ins = nc.vector.tensor_tensor(s_b[:, t * D:(t + 1) * D], bank[:, t * D:(t + 1) * D], b_p[:, :], ALU.add)
                    ins.then_inc(s.s_set, 1)
                    dve.wait_ge(s.s_set, b * 4 + (k + 1))
                    dve.wait_ge(s.gate_set, b * 4 + (k + 1))
                    nc.vector.scalar_tensor_tensor(s_b[:, :], s_b[:, :], 0.5 / SPIKE_STEPS, cnt[:, k, :],
                                                   ALU.mult, ALU.mult).then_inc(s.comb_link, 1)
                    dve.wait_ge(s.comb_link, b * 4 + (k + 1))
                    dve.wait_ge(s.x_again, b * 32 + 16 * (k // 2 + 1))
                    tiles = slice(2 * (k % 2), 2 * (k % 2) + 2)
                    nc.vector.tensor_tensor(x_out[:, tiles, :], s_b[:, :].rearrange("p (t d) -> p t d", t=2),
                                            x_out[:, tiles, :], ALU.add).then_inc(s.comb_set, 1)

                def row_maxima(b):
                    wait(dve, s.max_t, b)
                    for i in range(H * TT):
                        dve.wait_ge(s.max_scored, b * 128 + (i + 1))
                        nc.vector.tensor_reduce(row_max[:, i // TT, i % TT:i % TT + 1],
                                                scores[i % 2][:, :, :].rearrange("p a n -> p (a n)"), AX.X, ALU.max) \
                            .then_inc(s.max_set, 1)
                    dve.wait_ge(s.max_t, b + 1)
                    wait(dve, s.max_out, b * 16)
                    nc.vector.tensor_scalar(row_max_t, scores[0][:, 0, 0:P], -1.0, None, ALU.mult).then_inc(s.max_set, 1)

                def reduce_bounds():
                    dve.wait_ge(s.min_set, B * 2)
                    nc.vector.tensor_scalar(used[0:H, 3:4], c_min[:, 0:1], -CROW / (QS * QS * (R2MAX + SHIFT)), None, ALU.mult) \
                        .then_inc(used_set, 1)
                    dve.wait_ge(used_set, 5)
                    nc.vector.tensor_reduce(used_most[:, :], used[:, :], AX.X, ALU.max).then_inc(used_set, 1)

                def set_flag():
                    dve.wait_ge(flag_in, 16)
                    nc.vector.tensor_reduce(used_all[:, 0:1], used_all, AX.X, ALU.max).then_inc(flag_part, 1)
                    dve.wait_ge(flag_part, 1)
                    nc.vector.tensor_scalar(flag[:, :], used_all[:, 0:1], 1.0, None, ALU.is_gt).then_inc(flag_set, 1)

                if exact:
                    for stack in q_rows:
                        nc.vector.memset(stack[0:33, :, :], 0.0).then_inc(cleared, 1)
                    nc.vector.memset(pick_max, 0.0).then_inc(cleared, 1)
                    dve.wait_ge(cleared, 3)
                    nc.vector.memset(pick_max[32:33, :], 1.0).then_inc(cleared, 1)
                for t in range(TT):
                    ln_stats(0, t)
                for t in range(TT):
                    ln_apply(0, t)
                if not exact:
                    dve.wait_ge(wq_split, 1)
                    nc.vector.scalar_tensor_tensor(w_q16[:, 1, :, :], w_q[:, :, :], WS, w_q16[:, 0, :, :],
                                                   ALU.mult, ALU.subtract).then_inc(wq_split, 1)
                for n, (kind, k) in enumerate(prep_groups(exact)):
                    if kind == XT and not exact:
                        x_lo(0, k, aux[n % 2])
                    if kind == Q:
                        q_split(0, k, aux[n % 2])
                    if kind == C:
                        c_rows(0, k, aux[n % 2])
                if not exact:
                    dve.wait_ge(c_init, 1)
                    split_weights()
                    dve.wait_ge(norms, 1)
                    dve.wait_ge(used_set, 1)
                    nc.vector.tensor_reduce(used[0:1, 0:1], scores[0][0:1, :, :].rearrange("p a n -> p (a n)"),
                                            AX.X, ALU.max).then_inc(used_set, 1)
                    dve.wait_ge(squared, 3)
                    nc.vector.tensor_reduce(used[:, 1:2], proj_squares.rearrange("p k f -> p (k f)"), AX.X, ALU.max).then_inc(used_set, 1)
                    nc.vector.tensor_reduce(used[:, 2:3], wq_squares.rearrange("p k f -> p (k f)"), AX.X, ALU.max).then_inc(used_set, 1)
                    dve.wait_ge(used_set, 4)

                def body(b, first, last):
                    groups = batch_groups(first, last, exact)
                    _, done = schedule(groups)
                    if exact:
                        row_maxima(b)
                    tasks = []
                    for n, (offset, kind, k) in enumerate(groups):
                        at, bank = done[n], aux[n % 2]
                        if kind == FC:
                            tasks.append((at, n, relu, (b, k, bank)))
                        if kind == Y:
                            tasks.append((at, n, spikes, (b, k)))
                            if k < 3:
                                tasks.append((min(at + 4, STEPS), n, gate, (b, k)))
                        if kind == PROJ:
                            tasks.append((at, n, combine, (b + offset, k, bank)))
                        if kind == XT and not exact:
                            tasks.append((at, n, x_lo, (b + 1, k, bank)))
                        if kind == Q:
                            tasks.append((at, n, q_split, (b + 1, k, bank)))
                        if kind == C:
                            tasks.append((at, n, c_rows, (b + 1, k, bank)))
                    if not last:
                        for t in range(TT):
                            tasks.append((12 + t, -1, ln_stats, (b + 1, t)))
                            tasks.append((24 + t, -1, ln_apply, (b + 1, t)))
                    elif not exact:
                        tasks.append((0, -2, reduce_bounds, ()))
                        tasks.append((STEPS // 4, -1, set_flag, ()))
                    if not first:
                        tasks.append((0, -1, normalise, (b - 1, UNITS - 1)))
                        tasks.append((3, -1, gate, (b - 1, 3)))
                    for unit in range(UNITS - 1):
                        tasks.append((TT * (unit + 1), 100, normalise, (b, unit)))
                    for _, _, task, args in sorted(tasks, key=lambda task: task[:2]):
                        task(*args)

                batches(dve, body)
                normalise(B - 1, UNITS - 1)
                gate(B - 1, 3)
                for n, (kind, k) in enumerate(TAIL):
                    combine(B - 1, k, aux[n])

            run(bounded, False)
            in_general(dve, run)

        @block.gpsimd
        def _(pool):
            nc.gpsimd.memset(v_ones[:, :, :, :], 1.0).then_inc(v_set, 1)
            pool.wait_ge(v_set, 1)
            nc.gpsimd.memset(key_stack[64:65, :, :], CROW).then_inc(v_set, 1)
            pool.wait_ge(v_set, 2)
            def run(s, exact):
                def inv_std(b):
                    wait(pool, s.xn_set, b * 8)
                    wait_apart(pool, s.aggr_set, b * 8 + 8)
                    nc.gpsimd.tensor_scalar(var_eps[:, :], mean_var[:, :, 1], LN_EPS, None, ALU.add).then_inc(s.veps_set, 1)
                    pool.wait_ge(s.veps_set, b + 1)
                    nc.gpsimd.tensor_tensor(rstd[:, :], var_eps[:, :], minus_half[:, :], ALU.pow).then_inc(s.rstd_set, 1)

                def square_q(b, k):
                    chunk, half = k % 2, k // 2
                    cols = slice(half * HALF, (half + 1) * HALF)
                    pool.wait_ge(s.qhi_set, b * 4 + (k + 1))
                    wait(pool, s.pe_done[C], b * 2)
                    nc.gpsimd.tensor_tensor(q_sq[:, chunk, cols], q_hi[:, chunk, cols], q_hi[:, chunk, cols], ALU.mult).then_inc(s.sq_set, 1)

                def place_v(b, g):
                    wait(pool, s.pv_done, (b - 1) * 64 + (NG + g + 1) * TT)
                    wait_apart(pool, s.v_staged, b * 4 + 4)
                    at = 16 * (g % 2)
                    nc.gpsimd.tensor_copy(v_ones[:, :, G * g:G * g + G, at:at + DH],
                                          v_stage[:, :, G * g * DH:(G * g + G) * DH].rearrange("p t (h e) -> p t h e", h=G)).then_inc(s.vones_set, 1)

                def square_h(b, k):
                    f = k % KF
                    pool.wait_ge(s.relu_set, b * 16 + (k + 1))
                    wait(pool, s.pe_done[Y], b * 4 + (2 * (k // KF)))
                    tile = r[:, k % 2, :]
                    if exact:
                        nc.gpsimd.tensor_tensor(h_t[:, f, :], tile, tile, ALU.mult).then_inc(s.h_set, 1)
                        return
                    wait(pool, s.h_set, b * 16 + k)
                    nc.gpsimd.tensor_tensor(r_squared[:, :], tile, tile, ALU.mult).then_inc(s.rsq_set, 1)
                    pool.wait_ge(s.hhi_set, b * 16 + (k + 1))
                    pool.wait_ge(s.rsq_set, b * 16 + (k + 1))
                    nc.gpsimd.tensor_tensor(h_t16[:, 1, f, :], r_squared[:, :], h_t16[:, 0, f, :], ALU.subtract).then_inc(s.h_set, 1)

                pool.wait_ge(w_set, 2)
                inv_std(0)
                if not exact:
                    for n, (w, squares, bound, arrived) in enumerate(((fc_stage, fc_squares, W2MAX, (staged, 32)),
                                                                      (proj_stage, proj_squares, WMAX * WMAX, (staged, 32)),
                                                                      (w_q[:, :, :], wq_squares, WMAX * WMAX, (wq_in, H * 16)))):
                        pool.wait_ge(*arrived)
                        nc.gpsimd.tensor_scalar(squares, w, 1.0 / bound, None, ALU.mult).then_inc(square_link, 1)
                        pool.wait_ge(square_link, n + 1)
                        nc.gpsimd.tensor_tensor(squares, squares, w, ALU.mult).then_inc(squared, 1)
                if not exact:
                    for k in range(4):
                        square_q(0, k)
                pool.wait_ge(v_set, 2)
                for g in range(NG):
                    place_v(0, g)

                def body(b, first, last):
                    groups = batch_groups(first, last, exact)
                    _, done = schedule(groups)
                    tasks = []
                    for n, (offset, kind, k) in enumerate(groups):
                        if kind == FC:
                            tasks.append((done[n], square_h, (b, k)))
                        if kind == Q and not exact:
                            tasks.append((done[n], square_q, (b + 1, k)))
                        if (kind, k) == (V, 3):
                            tasks += [(max(done[n] + 1, TT * (NG + g + 1)), place_v, (b + 1, g)) for g in range(NG)]
                    if not last:
                        tasks.append((20, inv_std, (b + 1,)))
                    for _, task, args in sorted(tasks, key=lambda task: task[0]):
                        task(*args)

                batches(pool, body)

            run(bounded, False)
            in_general(pool, run)


def kernel(L0_attn_x, L0_attn_Wq, L0_attn_Wp, L0_attn_bp, L0_ffn_W_fc, L0_ffn_W_proj):
    import numpy as np
    import concourse.bacc as bacc
    from concourse.bass_utils import run_bass_kernel_spmd

    x, wq, wp, bp, wfc, wproj = (np.asarray(a) for a in (L0_attn_x, L0_attn_Wq, L0_attn_Wp, L0_attn_bp, L0_ffn_W_fc, L0_ffn_W_proj))
    wp_rows = wp.T.reshape(NG // 2, 2, G, DH, D)
    wp_s = wp_rows.transpose(2, 1, 3, 0, 4).reshape(P, NG // 2, D)
    ident = np.eye(P, dtype=np.float32)
    p = np.arange(P)
    head_sum = np.zeros((P, KD, H), np.float32)
    for k in range(KD):
        head_sum[p, k, 8 * k + p // DH] = 1.0
    arrays = {
        "x": x, "wq_t": wq.transpose(0, 2, 1), "wp_s": wp_s, "bp": bp,
        "wfc_t": wfc.T.reshape(KD, P, F).transpose(1, 0, 2),
        "wproj_t": wproj.T.reshape(KF, P, D).transpose(1, 0, 2),
        "consts": np.concatenate([ident, head_sum.reshape(P, -1), np.ones((P, 1), np.float32)], 1),
    }
    arrays = {k: np.ascontiguousarray(v) for k, v in arrays.items()}
    nc = bacc.Bacc("TRN2", target_bir_lowering=False, num_devices=1)
    args = {k: nc.dram_tensor(k, v.shape, FP32, kind="ExternalInput").ap() for k, v in arrays.items()}
    q_scratch = nc.dram_tensor("q_scratch", (H, 2, DH, N), FP16, kind="Internal").ap()
    c_scratch = nc.dram_tensor("c_scratch", (H, N), FP16, kind="Internal").ap()
    q_own_scratch = nc.dram_tensor("q_own_scratch", (H, DH, N), FP32, kind="Internal").ap()
    max_scratch = nc.dram_tensor("max_scratch", (P, P), FP32, kind="Internal").ap()
    bound_scratch = nc.dram_tensor("bound_scratch", (P, 1), FP32, kind="Internal").ap()
    out = nc.dram_tensor("out", (B, N, D), FP32, kind="ExternalOutput").ap()
    build(nc, **args, q_scratch=q_scratch, c_scratch=c_scratch, q_own_scratch=q_own_scratch,
          max_scratch=max_scratch, bound_scratch=bound_scratch, out=out)
    got = run_bass_kernel_spmd(nc, [arrays], core_ids=[0])
    return got.results[0]["out"]
```

```python
from contextlib import ExitStack

from concourse import mybir

FP32 = mybir.dt.float32
FP16 = mybir.dt.float16
BF16 = mybir.dt.bfloat16
INT32 = mybir.dt.int32
ALU = mybir.AluOpType
ACT = mybir.ActivationFunctionType
AX = mybir.AxisListType

B, N, D = 16, 1024, 256
H, DH = 16, 16
F = 4 * D
P = 128
TT = N // P
KD = D // P
KF = F // P
HALF = 512
NH = N // HALF
G = 4
NG = H // G
UNITS = NH * NG
STEPS = UNITS * TT
STRIP = P // G
LN_EPS = 1e-5
BETA, THRESHOLD, SPIKE_STEPS = 0.9, 1.0, 5

QS = 1024.0
SCORE_SCALE = 4.0 / (QS * QS)
TWO_CROW = 0x6C006C00
CROW = 4096.0
SHIFT = 15.5
R2MAX = 130.0

XS = 1024.0
WS = 4096.0
HS = 64.0
RS = 1024.0
WMAX = 15.0
W2MAX = 3.5


def spike_thresholds():
    import numpy as np

    def count(y):
        mem, spikes = np.float32(0), 0
        for _ in range(SPIKE_STEPS):
            reset = np.float32(mem - np.float32(THRESHOLD) > 0)
            mem = np.float32(np.float32(np.float32(BETA) * mem) + y) - reset * np.float32(THRESHOLD)
            spikes += int(mem - np.float32(THRESHOLD) > 0)
        return spikes

    found = []
    for k in range(1, SPIKE_STEPS + 1):
        low, high = 0, int(np.float32(64.0).view(np.int32))
        while high - low > 1:
            mid = (low + high) // 2
            low, high = (low, mid) if count(np.int32(mid).view(np.float32)) >= k else (mid, high)
        found.append(float(np.int32(high).view(np.float32)))
    return found


FC, Y, PROJ, XT, Q, C, V = "fc", "y", "proj", "xt", "q", "c", "v"
COST = {FC: 1.28, Y: 5.12, PROJ: 1.28, XT: 0.5, Q: 0.64, C: 0.43, V: 0.64}
COUNT = {FC: KF * NH, Y: TT // 2, PROJ: TT // 2, XT: KD * NH, Q: KD * NH, C: NH, V: TT // 2}
PREP = [(XT, k) for k in range(4)] + [(Q, k) for k in range(4)] + [(C, k) for k in range(2)] \
    + [(V, k) for k in range(4)]
TAIL = [(PROJ, k) for k in range(2, 4)]
PARTS = {FC: 2, Y: 16, PROJ: 4, XT: 1, Q: 1, C: 1, V: 1}


def prep_groups(exact):
    return [group for group in PREP if not (exact and group[0] == C)]


def batch_groups(first, last, exact):
    own = [(0, FC, k) for k in range(8)] + [(0, Y, k) for k in range(2)] + [(0, FC, k) for k in range(8, 16)]
    proj = [(0, PROJ, k) for k in range(2)]
    tail = [] if first else [(-1, kind, k) for kind, k in TAIL]
    prep = [] if last else [(1, kind, k) for kind, k in prep_groups(exact)]
    middle = prep[:1] + proj[:1] + prep[1:3] + proj[1:] + prep[3:]
    return own[:3] + tail + own[3:] + middle + [(0, Y, k) for k in range(2, 4)]


def schedule(groups):
    total = sum(COST[kind] for _, kind, _ in groups)
    at, step, out, done = 0.0, 0, [[] for _ in range(STEPS)], []
    for n, (offset, kind, k) in enumerate(groups):
        for part in range(PARTS[kind]):
            step = max(step, int(at / total * STEPS))
            if kind == PROJ:
                step = max(step, STEPS // 2 + 3 if offset == 0 else 3)
            step = min(step, STEPS - 1)
            out[step].append((kind, k, part, n))
            at += COST[kind] / PARTS[kind]
        done.append(step)
    return out, done


class Signals:

    def __init__(self, sem, way):
        self.x_in = sem(f"{way}_x_in")
        self.x_again = sem(f"{way}_x_again")
        self.out_done = sem(f"{way}_out_done")
        self.q_out = sem(f"{way}_q_out")
        self.c_out = sem(f"{way}_c_out")
        self.scored = sem(f"{way}_scored")
        self.pv_done = sem(f"{way}_pv_done")
        self.exp_done = sem(f"{way}_exp_done")
        self.xhi_set = sem(f"{way}_xhi_set")
        self.xnt_set = sem(f"{way}_xnt_set")
        self.v_staged = sem(f"{way}_v_staged")
        self.y_set = sem(f"{way}_y_set")
        self.th_set = sem(f"{way}_th_set")
        self.stat_set = sem(f"{way}_stat_set")
        self.aggr_set = sem(f"{way}_aggr_set")
        self.xn_set = sem(f"{way}_xn_set")
        self.relu_set = sem(f"{way}_relu_set")
        self.hhi_set = sem(f"{way}_hhi_set")
        self.fc_taken = self.hhi_set if way == "bounded" else self.relu_set
        self.qhi_set = sem(f"{way}_qhi_set")
        self.qlo_set = sem(f"{way}_qlo_set")
        self.c_set = sem(f"{way}_c_set")
        self.min_set = sem(f"{way}_min_set")
        self.cnt_link = sem(f"{way}_cnt_link")
        self.gate_set = sem(f"{way}_gate_set")
        self.acct_set = sem(f"{way}_acct_set")
        self.recip_set = sem(f"{way}_recip_set")
        self.scaled_set = sem(f"{way}_scaled_set")
        self.split_set = sem(f"{way}_split_set")
        self.res_set = sem(f"{way}_res_set")
        self.s_set = sem(f"{way}_s_set")
        self.comb_link = sem(f"{way}_comb_link")
        self.comb_set = sem(f"{way}_comb_set")
        self.veps_set = sem(f"{way}_veps_set")
        self.rstd_set = sem(f"{way}_rstd_set")
        self.rsq_set = sem(f"{way}_rsq_set")
        self.h_set = sem(f"{way}_h_set")
        self.sq_set = sem(f"{way}_sq_set")
        self.vones_set = sem(f"{way}_vones_set")
        self.max_scored = sem(f"{way}_max_scored")
        self.max_set = sem(f"{way}_max_set")
        self.max_t = sem(f"{way}_max_t")
        self.max_out = sem(f"{way}_max_out")
        self.max_in = sem(f"{way}_max_in")
        self.stack_in = [sem(f"{way}_stack_in{g}") for g in range(NG)]
        self.pe_done = {kind: sem(f"{way}_pe_{kind}") for kind in COUNT}


def build(nc, x, wq_t, wp_s, bp, wfc_t, wfc_rows, wproj_t, consts, q_scratch, c_scratch, q_own_scratch,
          max_scratch, bound_scratch, out):
    thresholds = spike_thresholds()
    x_v = x.rearrange("b (p t) d -> b p t d", p=P)
    out_v = out.rearrange("b (p t) d -> b p t d", p=P)

    ctx = ExitStack()
    with ctx:
        def sb(name, shape, dtype):
            return ctx.enter_context(nc.sbuf_tensor(name, shape, dtype))

        def sem(name):
            return ctx.enter_context(nc.semaphore(name))

        w_fc = sb("w_fc", [P, KD, F], FP32)
        w_proj = sb("w_proj", [P, KF, D], FP32)
        w_p = sb("w_p", [P, NG // 2, D], FP32)
        w_q = sb("w_q", [P, KD, P], FP32)
        w_q16 = sb("w_q16", [P, 2, KD, P], FP16)
        b_p = sb("b_p", [P, D], FP32)
        const = sb("const", [P, P + KD * H], FP32)
        ident = const[:, 0:P]
        head_sum = sb("head_sum", [P, KD, H], BF16)
        minus_half = sb("minus_half", [P, TT], FP32)
        x_tok = sb("x_tok", [P, TT, D], FP32)
        stats = sb("stats", [P, TT, 6], FP32)
        mean_var = sb("mean_var", [P, TT, 2], FP32)
        var_eps = sb("var_eps", [P, TT], FP32)
        rstd = sb("rstd", [P, TT], FP32)
        xn_t = sb("xn_t", [P, KD, N], FP32)
        q_hi = sb("q_hi", [P, KD, N], FP16)
        q_lo = sb("q_lo", [P, KD, N], FP16)
        q_sq = sb("q_sq", [P, KD, N], BF16)
        key_stack = sb("key_stack", [96 + H, H, N], FP16)
        key_row = key_stack[64:65, :, :].bitcast(INT32)
        c_row = key_stack[96:96 + H, 0, :]
        query_stack = sb("query_stack", [65, H, N], FP16)
        v_stage = sb("v_stage", [P, TT, D], FP32)
        v_ones = sb("v_ones", [P, TT, H, STRIP], FP32)
        NE = 4
        e = sb("e", [P, NE, 2, HALF], FP32)
        acc_t = sb("acc_t", [P, HALF // STRIP, STRIP], FP32)
        recip = sb("recip", [P, HALF // STRIP, 1], FP32)
        scaled_t = sb("scaled_t", [P, HALF // STRIP, STRIP], FP32)
        res = sb("res", [P, NH, NG // 2, HALF], FP32)
        r = sb("r", [P, 2, HALF], FP32)
        r_squared = sb("r_squared", [P, HALF], FP32)
        h_t = sb("h_t", [P, KF, HALF], FP32)
        y_sb = sb("y_sb", [P, 2, HALF], FP32)

        def halves(tensor):
            flat = tensor[:, :, :].rearrange("p a b -> p (a b)").bitcast(FP16)
            return flat.rearrange("p (s a b) -> p s a b", s=2, a=tensor.shape[1])

        w_fc16, w_proj16, w_p16, xn_t16, h_t16, scaled_t16 = (halves(t) for t in (w_fc, w_proj, w_p, xn_t, h_t, acc_t))
        res16 = res[:, :, :, :].rearrange("p h g n -> p (h g n)").bitcast(FP16).rearrange("p (s h g n) -> p s h g n", s=2, h=NH, g=NG // 2)
        cnt = sb("cnt", [P, TT // 2, HALF], FP32)
        x_out = sb("x_out", [P, TT // NH, D], FP32)
        s_b = sb("s_b", [P, HALF], FP32)
        c_min = sb("c_min", [H, 2], FP32)
        used = sb("used", [P, 5], FP32)
        used_most = sb("used_most", [P, 1], FP32)
        flag = sb("flag", [1, 1], INT32)
        used_all = x_tok[0:1, 0, 0:P]
        q_own = x_tok[:, :, :].rearrange("p t d -> p (t d)").rearrange("p (k n) -> p k n", k=KD)
        q_rows = [stack[0:65, :, :].bitcast(FP32) for stack in (key_stack, query_stack)]
        pick_max = q_hi[0:33, 0, 0:2 * P].bitcast(FP32)
        row_max = q_sq[:, 0, 0:2 * H * TT].bitcast(FP32).rearrange("p (h t) -> p h t", h=H)
        row_max_t = q_sq[:, 1, 0:2 * P].bitcast(FP32)

        scores = [ctx.enter_context(nc.psum_tensor(f"scores{i}", [P, 2, HALF], FP32)) for i in range(2)]
        acc = [ctx.enter_context(nc.psum_tensor(f"acc{i}", [P, HALF], FP32)) for i in range(2)]
        aux = [ctx.enter_context(nc.psum_tensor(f"aux{i}", [P, HALF], FP32)) for i in range(2)]

        fc_stage = cnt[:, :, :].rearrange("p a n -> p (a n)").rearrange("p (k f) -> p k f", k=KD)
        proj_stage = res[:, :, :, :].rearrange("p a b n -> p (a b n)").rearrange("p (k f) -> p k f", k=KF)
        wp_stage = s_b[:, :].rearrange("p (g d) -> p g d", g=NG // 2)
        fc_rows, proj_again = x_tok, v_stage
        row_norms = var_eps
        wp_again = q_lo[:, 0, :].bitcast(FP32)
        wq_squares = q_hi[:, 0, 0:2 * KD * P].bitcast(FP32)

        w_in, wq_in, w_set, v_set = sem("w_in"), sem("wq_in"), sem("w_set"), sem("v_set")
        fc_staged, proj_staged, w_again = sem("fc_staged"), sem("proj_staged"), sem("w_again")
        wq_split, fc_split, proj_split = sem("wq_split"), sem("fc_split"), sem("proj_split")
        wp_split = sem("wp_split")
        checks_in, squared, used_set, key_row_set = sem("checks_in"), sem("squared"), sem("used_set"), sem("key_row_set")
        c_init, const_in = sem("c_init"), sem("const_in")
        flag_part, flag_out, flag_in, flag_set = sem("flag_part"), sem("flag_out"), sem("flag_in"), sem("flag_set")
        cleared = sem("cleared")
        bounded, general = Signals(sem, "bounded"), Signals(sem, "general")

        def wait(eng, semaphore, value):
            if not (isinstance(value, int) and value <= 0):
                eng.wait_ge(semaphore, value)

        def wait_apart(eng, semaphore, value):
            wait(eng, semaphore, value)
            eng.nop(nofuse=True)

        def emptied(s, kind, b, k):
            return {FC: (s.fc_taken, b * 16 + (k + 1)), Y: (s.y_set, b * 4 + (k + 1)), PROJ: (s.s_set, b * 4 + (k + 1)),
                    XT: (s.xnt_set, b * 4 + (k + 1)), Q: (s.qlo_set, b * 4 + (k + 1)), C: (s.c_set, b * 2 + (k + 1)),
                    V: (s.v_staged, b * 4 + (k + 1))}[kind]

        block = ctx.enter_context(nc.Block())

        def batches(eng, body):
            body(0, True, False)
            with nc.Fori(1, B - 1, engines=(eng.engine,), hint_back_edge=True) as b:
                body(b, False, False)
            body(B - 1, False, True)

        def in_general(eng, run):
            eng.wait_ge(bounded.out_done, B * 32)
            eng.wait_ge(flag_set, 1)
            beyond = eng.value_load(flag[0:1, 0:1], min_val=0, max_val=1)
            with eng.If(beyond > 0):
                run(general, True)

        @block.sync
        def _(sp):
            sp.dma_start(x_tok[:, :, :], x_v[0, :, :, :]).then_inc(bounded.x_in, 16)
            sp.dma_start(const[:, :], consts).then_inc(const_in, 16)
            sp.wait_ge(w_set, 1)
            for h in range(H):
                p = DH * h % P
                sp.dma_start(w_q[p:p + DH, h // 8, p:p + DH], wq_t[h, :, :]).then_inc(wq_in, 16)
            sp.dma_start(fc_stage, wfc_t).then_inc(fc_staged, 16)
            sp.dma_start(proj_stage, wproj_t).then_inc(proj_staged, 16)
            for dst, src in ((wp_stage, wp_s), (b_p[:, :], bp.rearrange("(a d) -> a d", a=1).broadcast_to((P, D)))):
                sp.dma_start(dst, src).then_inc(w_in, 16)

            def run(s, exact):
                stack_loads = 16 * (2 if exact else 7)

                def load_x(b):
                    wait_apart(sp, s.pe_done[XT], b * 4)
                    if exact:
                        wait(sp, s.q_out, b * 32)
                    sp.dma_start(x_tok[:, :, :], x_v[b, :, :, :]).then_inc(s.x_in, 16)

                def store_q(b):
                    wait_apart(sp, s.qlo_set, b * 4 + 4)
                    for g in range(NG):
                        wait_apart(sp, s.stack_in[g], b * stack_loads)
                    if exact:
                        for k in range(KD):
                            sp.dma_start(q_own_scratch[8 * k:8 * k + 8, :, :], q_own[:, k, :]).then_inc(s.q_out, 16)
                        wait_apart(sp, s.q_out, b * 32 + 32)
                        return
                    for part, q in enumerate((q_hi, q_lo)):
                        for k in range(KD):
                            sp.dma_start(q_scratch[8 * k:8 * k + 8, part, :, :], q[:, k, :]).then_inc(s.q_out, 16)
                    sp.wait_ge(s.c_set, b * 2 + 2)
                    sp.dma_start(c_scratch, c_row).then_inc(s.c_out, 16)
                    wait_apart(sp, s.q_out, b * 64 + 64)
                    wait_apart(sp, s.c_out, b * 16 + 16)

                def load_stack(b, g):
                    wait_apart(sp, s.scored, (b - 1) * 128 + (NG + g + 1) * 16)
                    heads = slice(G * g, G * g + G)
                    if exact:
                        for half in range(NH):
                            sp.dma_start(q_rows[half][0:DH, heads, :],
                                         q_own_scratch[heads, :, half * HALF:(half + 1) * HALF].rearrange("h e n -> e h n")) \
                                .then_inc(s.stack_in[g], 16)
                        return
                    for rep in range(2):
                        sp.dma_start(query_stack[32 * rep:32 * rep + 32, heads, :],
                                     q_scratch[heads, :, :, :].rearrange("h s e n -> (s e) h n")).then_inc(s.stack_in[g], 16)
                        for part in range(2):
                            row = 32 * part + 16 * rep
                            sp.dma_start(key_stack[row:row + 16, heads, :],
                                         q_scratch[heads, part, :, :].rearrange("h e n -> e h n")).then_inc(s.stack_in[g], 16)
                    sp.dma_start(query_stack[64:65, heads, :],
                                 c_scratch[heads, :].rearrange("(a h) n -> a h n", a=1)).then_inc(s.stack_in[g], 16)

                def store_out(b, half):
                    sp.wait_ge(s.comb_set, b * 4 + (2 * half + 2))
                    sp.dma_start(out_v[b, :, 4 * half:4 * half + 4, :], x_out[:, :, :]).then_inc(s.out_done, 16)

                def load_again(b, half):
                    wait(sp, s.out_done, b * 32 + 16 * half)
                    sp.dma_start(x_out[:, :, :], x_v[b, :, 4 * half:4 * half + 4, :]).then_inc(s.x_again, 16)

                def place_max(b):
                    sp.wait_ge(s.max_set, b * 129 + 129)
                    sp.dma_start(max_scratch, row_max_t).then_inc(s.max_out, 16)
                    wait_apart(sp, s.max_out, b * 16 + 16)
                    wait(sp, s.scored, b * 128)
                    for half in range(NH):
                        sp.dma_start(q_rows[half][32:33, :, :],
                                     max_scratch.rearrange("(a h s t) n -> s a h (t n)", a=1, h=H, s=NH)[half]).then_inc(s.max_in, 16)

                def load_checks():
                    sp.wait_ge(s.pe_done[XT], B * 4)
                    sp.dma_start(fc_rows[:, :, :], wfc_rows.rearrange("(k p) d -> p k d", p=P)).then_inc(checks_in, 16)
                    sp.wait_ge(s.vones_set, B * 4)
                    sp.dma_start(proj_again[:, :, :], wproj_t).then_inc(checks_in, 16)
                    sp.wait_ge(s.q_out, B * 64)
                    sp.dma_start(wp_again, wp_s.rearrange("p g d -> p (g d)")).then_inc(checks_in, 16)

                def collect_bound():
                    sp.wait_ge(used_set, 10)
                    sp.dma_start(bound_scratch, used_most[:, :]).then_inc(flag_out, 16)
                    sp.wait_ge(flag_out, 16)
                    sp.dma_start(used_all, bound_scratch.rearrange("p a -> a p")).then_inc(flag_in, 16)

                if exact:
                    load_x(0)
                    for dst, src in ((w_fc[:, :, :], wfc_t), (w_proj[:, :, :], wproj_t), (w_p[:, :, :], wp_s)):
                        sp.dma_start(dst, src).then_inc(w_again, 16)
                store_q(0)
                if exact:
                    sp.wait_ge(cleared, 4)
                for g in range(NG):
                    load_stack(0, g)

                def body(b, first, last):
                    if exact:
                        place_max(b)
                    elif last:
                        load_checks()
                    if not last:
                        load_x(b + 1)
                    if not first:
                        store_out(b - 1, 1)
                    load_again(b, 0)
                    if last and not exact:
                        collect_bound()
                    store_out(b, 0)
                    load_again(b, 1)
                    if not last:
                        store_q(b + 1)
                        for g in range(NG):
                            load_stack(b + 1, g)

                batches(sp, body)
                store_out(B - 1, 1)
                sp.wait_ge(s.out_done, B * 32)

            run(bounded, False)
            in_general(sp, run)

        @block.tensor
        def _(pe):
            def run(s, exact):
                def product(out, a, b, first=True, last=True):
                    for n, (x, y) in enumerate(((0, 0), (0, 1), (1, 0))):
                        ins = nc.tensor.matmul(out, a(x), b(y), start=first and n == 0, stop=last and n == 2)
                    return ins

                def paired(b, kind, k, part, bank):
                    half = k // KF if kind == FC else k // 2
                    cols = slice(half * HALF, (half + 1) * HALF)
                    if kind == FC:
                        f = k % KF
                        return product(bank[:, :], lambda x: w_fc16[:, x, part, f * P:(f + 1) * P],
                                       lambda x: xn_t16[:, x, part, cols], part == 0, part == 1)
                    if kind == Y:
                        t, f = part // KF, part % KF
                        if part < KF:
                            pe.wait_ge(s.h_set, b * 16 + (8 * half + f + 1))
                        col = (2 * k + t) % 4 * P
                        return product(bank[:, t * D:(t + 1) * D], lambda x: h_t16[:, x, f, col:col + P],
                                       lambda x: w_proj16[:, x, f, :], f == 0, f == KF - 1)
                    if kind == PROJ:
                        t, pair = part // 2, part % 2
                        if part == 0:
                            pe.wait_ge(s.res_set, b * 8 + (4 * half + 4))
                        col = (2 * k + t) % 4 * P
                        return product(bank[:, t * D:(t + 1) * D], lambda x: res16[:, x, half, pair, col:col + P],
                                       lambda x: w_p16[:, x, pair, :], pair == 0, pair == 1)
                    if kind == Q:
                        chunk = k % 2
                        pe.wait_ge(s.xnt_set, b * 4 + (k + 1))
                        return product(bank[:, :], lambda x: w_q16[:, x, chunk, :], lambda x: xn_t16[:, x, chunk, cols])
                    for t in range(2):
                        for chunk in range(KD):
                            tokens = slice((2 * k + t) * P, (2 * k + t + 1) * P)
                            ins = product(bank[:, t * D + chunk * P:t * D + (chunk + 1) * P],
                                          lambda x: xn_t16[:, x, chunk, tokens], lambda x: w_q16[:, x, chunk, :])
                    return ins

                def aux_part(b, piece, before):
                    kind, k, part, n = piece
                    bank = aux[n % 2]
                    if part == 0:
                        wait(pe, *before)
                    if not exact and kind in (FC, Y, PROJ, Q, V):
                        ins = paired(b, kind, k, part, bank)
                    elif kind == FC:
                        half, f = k // KF, k % KF
                        ins = nc.tensor.matmul(bank[:, :], w_fc[:, part, f * P:(f + 1) * P],
                                               xn_t[:, part, half * HALF:(half + 1) * HALF], start=part == 0, stop=part == 1)
                    elif kind == Y:
                        t, f = part // KF, part % KF
                        if part < KF:
                            pe.wait_ge(s.h_set, b * 16 + (8 * (k // 2) + f + 1))
                        col = (2 * k + t) % 4 * P
                        ins = nc.tensor.matmul(bank[:, t * D:(t + 1) * D], h_t[:, f, col:col + P], w_proj[:, f, :],
                                               start=f == 0, stop=f == KF - 1)
                    elif kind == PROJ:
                        t, pair = part // 2, part % 2
                        half = k // 2
                        if part == 0:
                            pe.wait_ge(s.res_set, b * 8 + (4 * half + 4))
                        col = (2 * k + t) % 4 * P
                        ins = nc.tensor.matmul(bank[:, t * D:(t + 1) * D], res[:, half, pair, col:col + P], w_p[:, pair, :],
                                               start=pair == 0, stop=pair == 1)
                    elif kind == XT:
                        chunk, half = k % 2, k // 2
                        pe.wait_ge(s.xn_set, b * 8 + (4 * half + 4))
                        for t in range(4):
                            ins = nc.tensor.transpose(bank[:, t * P:(t + 1) * P],
                                                      x_tok[:, 4 * half + t, chunk * P:(chunk + 1) * P], ident)
                    elif kind == Q:
                        chunk, half = k % 2, k // 2
                        pe.wait_ge(s.xnt_set, b * 4 + (k + 1))
                        ins = nc.tensor.matmul(bank[:, :], w_q[:, chunk, :], xn_t[:, chunk, half * HALF:(half + 1) * HALF],
                                               start=True, stop=True)
                    elif kind == C:
                        pe.wait_ge(s.sq_set, b * 4 + (2 * k + 2))
                        for chunk in range(KD):
                            ins = nc.tensor.matmul(bank[0:H, :], head_sum[:, chunk, :], q_sq[:, chunk, k * HALF:(k + 1) * HALF],
                                                   start=chunk == 0, stop=chunk == KD - 1)
                    else:
                        for t in range(2):
                            for chunk in range(KD):
                                ins = nc.tensor.matmul(bank[:, t * D + chunk * P:t * D + (chunk + 1) * P],
                                                       xn_t[:, chunk, (2 * k + t) * P:(2 * k + t + 1) * P],
                                                       w_q[:, chunk, :], start=True, stop=True)
                    if part == PARTS[kind] - 1:
                        ins.then_inc(s.pe_done[kind], 1)

                def pv(b, i):
                    unit, j = i // TT, i % TT
                    half, g = unit // NG, unit % NG
                    if j == 0:
                        wait(pe, s.acct_set, b * 8 + (unit - 1))
                        if half == 0:
                            pe.wait_ge(s.vones_set, b * 4 + (g + 1))
                    pe.wait_ge(s.exp_done, b * 128 + (2 * i + 2))
                    for n in range(G):
                        tile = (2 * i + n // 2) % NE
                        ins = nc.tensor.matmul(acc[unit % 2][STRIP * n:STRIP * (n + 1), :], v_ones[:, j, G * g + n, :],
                                               e[:, tile, n % 2, :], start=j == 0, stop=j == TT - 1)
                    ins.then_inc(s.pv_done, 1)

                def row_maxima(b):
                    for g in range(NG):
                        pe.wait_ge(s.stack_in[g], b * 32 + 32)
                    for i in range(H * TT):
                        head, t = i // TT, i % TT
                        if i >= 2:
                            pe.wait_ge(s.max_set, b * 129 + (i - 1))
                        for half in range(NH):
                            ins = nc.tensor.matmul(scores[i % 2][:, half, :],
                                                   q_rows[t // 4][0:DH, head, t % 4 * P:(t % 4 + 1) * P],
                                                   q_rows[half][0:DH, head, :], start=True, stop=True)
                        ins.then_inc(s.max_scored, 1)
                    pe.wait_ge(s.max_set, b * 129 + 128)
                    nc.tensor.transpose(scores[0][:, 0, 0:P], row_max[:, :, :].rearrange("p h t -> p (h t)"), ident) \
                        .then_inc(s.max_t, 1)
                    pe.wait_ge(s.max_in, b * 32 + 32)

                def score(bank, head, half, j):
                    if not exact:
                        return nc.tensor.matmul(bank, key_stack[0:65, head, j * P:(j + 1) * P],
                                                query_stack[:, head, half * HALF:(half + 1) * HALF], start=True, stop=True)
                    nc.tensor.matmul(bank, q_rows[j // 4][0:DH, head, j % 4 * P:(j % 4 + 1) * P],
                                     q_rows[half][0:DH, head, :], start=True, stop=False)
                    return nc.tensor.matmul(bank, pick_max, q_rows[half][0:33, head, :], start=False, stop=True)

                pe.wait_ge(const_in, 16)
                pe.wait_ge(wq_split, 2)
                pe.wait_ge(w_set, 3)
                for n, (kind, k) in enumerate(prep_groups(exact)):
                    before = emptied(s, prep_groups(exact)[n - 2][0], 0, prep_groups(exact)[n - 2][1]) if n >= 2 else (w_in, 0)
                    aux_part(0, (kind, k, 0, n), before)
                pe.wait_ge(key_row_set, 1)
                pe.wait_ge(v_set, 2)
                pe.wait_ge(w_in, 2 * 16)
                if exact:
                    pe.wait_ge(cleared, 4)
                    pe.wait_ge(w_again, 3 * 16)

                def body(b, first, last):
                    groups = batch_groups(first, last, exact)
                    steps, _ = schedule(groups)
                    order = ([(0, V, 2), (0, V, 3)] if first else [(b - 1, Y, 2), (b - 1, Y, 3)]) \
                        + [(b + offset, kind, k) for offset, kind, k in groups]
                    if exact:
                        wait(pe, s.exp_done, b * 128)
                        row_maxima(b)
                    for i in range(STEPS):
                        unit, j = i // TT, i % TT
                        half, g = unit // NG, unit % NG
                        if j == 0 and half == 0 and not exact:
                            pe.wait_ge(s.stack_in[g], b * 112 + 112)
                        for pair in range(2):
                            tile = 2 * i + pair
                            wait(pe, s.exp_done, b * 128 + (tile - 1))
                            for n in range(2):
                                head = G * g + 2 * pair + n
                                ins = score(scores[tile % 2][:, n, :], head, half, j)
                            ins.then_inc(s.scored, 1)
                        if i:
                            pv(b, i - 1)
                        elif not first:
                            pv(b - 1, STEPS - 1)
                        for piece in steps[i]:
                            n = piece[3]
                            if first and not exact and piece[:3] == (FC, 0, 0):
                                pe.wait_ge(fc_split, 2)
                            if first and not exact and piece[:3] == (Y, 0, 0):
                                pe.wait_ge(proj_split, 2)
                            if first and not exact and piece[:3] == (PROJ, 0, 0):
                                pe.wait_ge(wp_split, 2)
                            aux_part(order[n + 2][0], piece, emptied(s, order[n][1], order[n][0], order[n][2]))

                batches(pe, body)
                pv(B - 1, STEPS - 1)
                for n, (kind, k) in enumerate(TAIL):
                    for part in range(PARTS[kind]):
                        aux_part(B - 1, (kind, k, part, n), emptied(s, Y, B - 1, 2 + n))

            run(bounded, False)
            in_general(pe, run)

        @block.scalar
        def _(act):
            def run(s, exact):
                def evac(b, kind, k, bank):
                    if kind == XT:
                        chunk, half = k % 2, k // 2
                        wait(act, s.pe_done[FC], b * 16)
                        wait(act, s.pe_done[V], b * 4)
                        act.wait_ge(s.pe_done[XT], b * 4 + (k + 1))
                        if not exact:
                            nc.scalar.activation(xn_t16[:, 0, chunk, half * HALF:(half + 1) * HALF], bank[:, :], ACT.Copy,
                                                 scale=XS).then_inc(s.xhi_set, 1)
                            return
                        nc.scalar.activation(xn_t[:, chunk, half * HALF:(half + 1) * HALF], bank[:, :], ACT.Copy).then_inc(s.xnt_set, 1)
                    elif kind == V:
                        wait(act, s.vones_set, b * 4)
                        act.wait_ge(s.pe_done[V], b * 4 + (k + 1))
                        nc.scalar.activation(v_stage[:, 2 * k:2 * k + 2, :], bank[:, :].rearrange("p (t d) -> p t d", t=2),
                                             ACT.Copy, scale=1.0 if exact else 1.0 / (XS * WS)).then_inc(s.v_staged, 1)
                    elif kind == Y:
                        wait(act, s.gate_set, b * 4 + (k - 1))
                        act.wait_ge(s.pe_done[Y], b * 4 + (k + 1))
                        nc.scalar.activation(y_sb[:, k % 2, :], bank[:, :], ACT.Copy, scale=1.0 if exact else 1.0 / (HS * WS)).then_inc(s.y_set, 1)

                def tanh(b, k):
                    act.wait_ge(s.cnt_link, b * 20 + (k + 1) * 5)
                    nc.scalar.activation(y_sb[:, k % 2, :], cnt[:, k, :], ACT.Tanh, scale=0.5 / SPIKE_STEPS).then_inc(s.th_set, 1)

                if not exact:
                    act.wait_ge(wq_in, H * 16)
                    nc.scalar.activation(w_q16[:, 0, :, :], w_q[:, :, :], ACT.Copy, scale=WS).then_inc(wq_split, 1)
                for n, (kind, k) in enumerate(prep_groups(exact)):
                    if (kind, k) == (V, 0) and not exact:
                        act.wait_ge(fc_staged, 16)
                        nc.scalar.activation(w_fc16[:, 0, :, :], fc_stage, ACT.Copy, scale=WS).then_inc(fc_split, 1)
                    if kind in (XT, V):
                        evac(0, kind, k, aux[n % 2])


                def split_proj():
                    act.wait_ge(proj_staged, 16)
                    nc.scalar.activation(w_proj16[:, 0, :, :], proj_stage, ACT.Copy, scale=WS).then_inc(proj_split, 1)
                    act.wait_ge(w_in, 2 * 16)
                    nc.scalar.activation(w_p16[:, 0, :, :], wp_stage, ACT.Copy, scale=WS).then_inc(wp_split, 1)

                def body(b, first, last):
                    groups = batch_groups(first, last, exact)
                    _, done = schedule(groups)
                    tasks = []
                    for n, (offset, kind, k) in enumerate(groups):
                        if kind in (XT, V, Y):
                            tasks.append((done[n], n, evac, (b + offset, kind, k, aux[n % 2])))
                        if kind == Y and k < 3:
                            tasks.append((min(done[n] + 4, STEPS), n, tanh, (b, k)))
                    if not first:
                        tasks.append((1, -1, tanh, (b - 1, 3)))
                    elif not exact:
                        tasks.append((1, -1, split_proj, ()))
                    tasks.sort(key=lambda task: task[:2])
                    for i in range(STEPS + 1):
                        if i < STEPS:
                            for tile in (2 * i, 2 * i + 1):
                                act.wait_ge(s.scored, b * 128 + (tile + 1))
                                wait(act, s.pv_done, b * 64 + (tile // 2 - NE // 2 + 1))
                                nc.scalar.activation(e[:, tile % NE, :, :], scores[tile % 2][:, :, :], ACT.Exp,
                                                     scale=4.0 if exact else SCORE_SCALE).then_inc(s.exp_done, 1)
                        for at, _, task, args in tasks:
                            if at == i:
                                task(*args)

                batches(act, body)
                tanh(B - 1, 3)

            run(bounded, False)
            in_general(act, run)

        @block.vector
        def _(dve):
            nc.vector.memset(w_q[:, :, :], 0.0).then_inc(w_set, 1)
            nc.vector.memset(minus_half[:, :], -0.5).then_inc(w_set, 1)
            nc.vector.memset(key_row[:, 0:H // 2, :], TWO_CROW).then_inc(key_row_set, 1)
            dve.wait_ge(const_in, 16)
            nc.vector.tensor_copy(head_sum[:, :, :], const[:, P:P + KD * H].rearrange("p (k h) -> p k h", k=KD)).then_inc(w_set, 1)
            nc.vector.memset(c_min[:, :], 0.0).then_inc(c_init, 1)
            nc.vector.memset(used[:, :], 0.0).then_inc(used_set, 1)

            def run(s, exact):
                def ln_stats(b, t):
                    if t == 0:
                        dve.wait_ge(s.x_in, b * 16 + 16)
                        wait(dve, s.xn_set, b * 8)
                    nc.vector.bn_stats(stats[:, t, :], x_tok[:, t, :]).then_inc(s.stat_set, 1)
                    if t == TT - 1:
                        wait_apart(dve, s.rstd_set, b)
                        wait_apart(dve, s.stat_set, b * 8 + 8)
                        for u in range(TT):
                            nc.vector.bn_aggr(mean_var[:, u, :], stats[:, u, :]).then_inc(s.aggr_set, 1)

                def ln_apply(b, t):
                    dve.wait_ge(s.rstd_set, b + 1)
                    nc.vector.tensor_scalar(x_tok[:, t, :], x_tok[:, t, :], mean_var[:, t, 0:1], rstd[:, t:t + 1],
                                            ALU.subtract, ALU.mult).then_inc(s.xn_set, 1)

                def q_split(b, k, bank):
                    chunk, half = k % 2, k // 2
                    cols = slice(half * HALF, (half + 1) * HALF)
                    dve.wait_ge(s.pe_done[Q], b * 4 + (k + 1))
                    if exact:
                        nc.vector.tensor_scalar(q_own[:, chunk, cols], bank[:, :], 1.0, None, ALU.mult).then_inc(s.qlo_set, 1)
                        return
                    wait(dve, s.q_out, b * 64)
                    wait(dve, s.sq_set, b * 4)
                    nc.vector.tensor_scalar(q_hi[:, chunk, cols], bank[:, :], QS / (XS * WS), None, ALU.mult).then_inc(s.qhi_set, 1)
                    dve.wait_ge(s.qhi_set, b * 4 + (k + 1))
                    nc.vector.scalar_tensor_tensor(q_lo[:, chunk, cols], bank[:, :], QS / (XS * WS), q_hi[:, chunk, cols],
                                                   ALU.mult, ALU.subtract).then_inc(s.qlo_set, 1)

                def c_rows(b, k, bank):
                    dve.wait_ge(s.pe_done[C], b * 2 + (k + 1))
                    wait(dve, s.c_out, b * 16)
                    wait(dve, s.min_set, b * 2)
                    nc.vector.tensor_scalar(c_row[:, k * HALF:(k + 1) * HALF], bank[0:H, :], -1.0 / CROW,
                                            -SHIFT * QS * QS / CROW, ALU.mult, ALU.add).then_inc(s.c_set, 1)
                    if k == NH - 1:
                        dve.wait_ge(s.c_set, b * 2 + 2)
                        nc.vector.tensor_reduce(c_min[:, 1:2], c_row, AX.X, ALU.min).then_inc(s.min_set, 1)
                        dve.wait_ge(s.min_set, b * 2 + 1)
                        nc.vector.tensor_tensor(c_min[:, 0:1], c_min[:, 0:1], c_min[:, 1:2], ALU.min).then_inc(s.min_set, 1)

                def x_lo(b, k, bank):
                    chunk, half = k % 2, k // 2
                    cols = slice(half * HALF, (half + 1) * HALF)
                    dve.wait_ge(s.xhi_set, b * 4 + (k + 1))
                    nc.vector.scalar_tensor_tensor(xn_t16[:, 1, chunk, cols], bank[:, :], XS, xn_t16[:, 0, chunk, cols],
                                                   ALU.mult, ALU.subtract).then_inc(s.xnt_set, 1)

                def split_lo(w16, stage, split):
                    dve.wait_ge(split, 1)
                    nc.vector.scalar_tensor_tensor(w16[:, 1, :, :], stage, WS, w16[:, 0, :, :],
                                                   ALU.mult, ALU.subtract).then_inc(split, 1)
                    dve.wait_ge(split, 2)

                def relu(b, k, bank):
                    dve.wait_ge(s.pe_done[FC], b * 16 + (k + 1))
                    wait(dve, s.h_set, b * 16 + (k - 1))
                    nc.vector.tensor_scalar(r[:, k % 2, :], bank[:, :], 0.0, 1.0 if exact else HS ** 0.5 / (XS * WS),
                                            ALU.max, ALU.mult).then_inc(s.relu_set, 1)
                    if exact:
                        return
                    wait(dve, s.pe_done[Y], b * 4 + (2 * (k // KF)))
                    dve.wait_ge(s.relu_set, b * 16 + (k + 1))
                    nc.vector.scalar_tensor_tensor(h_t16[:, 0, k % KF, :], bank[:, :], HS ** 0.5 / (XS * WS), r[:, k % 2, :],
                                                   ALU.mult, ALU.mult).then_inc(s.hhi_set, 1)

                def spikes(b, k):
                    dve.wait_ge(s.y_set, b * 4 + (k + 1))
                    wait(dve, s.comb_link, (b - 1) * 4 + k + 1)
                    link = b * 20 + k * 5
                    nc.vector.tensor_scalar(cnt[:, k, :], y_sb[:, k % 2, :], thresholds[0], None, ALU.is_ge).then_inc(s.cnt_link, 1)
                    for n in range(1, SPIKE_STEPS):
                        dve.wait_ge(s.cnt_link, link + n)
                        nc.vector.scalar_tensor_tensor(cnt[:, k, :], y_sb[:, k % 2, :], thresholds[n], cnt[:, k, :],
                                                       ALU.is_ge, ALU.add).then_inc(s.cnt_link, 1)

                def gate(b, k):
                    dve.wait_ge(s.th_set, b * 4 + (k + 1))
                    nc.vector.scalar_tensor_tensor(cnt[:, k, :], y_sb[:, k % 2, :], 1.0, cnt[:, k, :], ALU.add, ALU.mult).then_inc(s.gate_set, 1)

                def normalise(b, unit):
                    pair, odd = unit // 2, unit % 2
                    own, sums = (slice(DH, STRIP), 0) if odd else (slice(0, DH), DH)
                    wait(dve, s.scaled_set, b * 8 + unit)
                    if not odd:
                        wait(dve, s.res_set, b * 8 + 2 * pair)
                    dve.wait_ge(s.pv_done, b * 64 + (unit + 1) * TT)
                    nc.vector.transpose(acc_t[:, :, :].rearrange("p c r -> p (c r)"), acc[unit % 2][:, :]).then_inc(s.acct_set, 1)
                    dve.wait_ge(s.acct_set, b * 8 + (unit + 1))
                    nc.vector.reciprocal(recip[:, :, :], acc_t[:, :, sums:sums + 1]).then_inc(s.recip_set, 1)
                    if not odd:
                        wait(dve, s.res_set, b * 8 + 2 * pair)
                    dve.wait_ge(s.recip_set, b * 8 + (unit + 1))
                    nc.vector.tensor_tensor(scaled_t[:, :, own], acc_t[:, :, own],
                                            recip[:, :, :].broadcast_to((P, HALF // STRIP, DH)), ALU.mult).then_inc(s.scaled_set, 1)
                    if odd:
                        wait(dve, s.pe_done[PROJ], (b - 1) * 4 + (2 * (pair // 2) + 2))
                        dve.wait_ge(s.scaled_set, b * 8 + (unit + 1))
                        if exact:
                            nc.vector.transpose(res[:, pair // 2, pair % 2, :],
                                                scaled_t[:, :, :].rearrange("p c r -> p (c r)")).then_inc(s.res_set, 2)
                            return
                        nc.vector.tensor_scalar(scaled_t16[:, 0, :, :], scaled_t[:, :, :], RS, None, ALU.mult).then_inc(s.split_set, 1)
                        dve.wait_ge(s.split_set, b * 8 + (2 * pair + 1))
                        nc.vector.scalar_tensor_tensor(scaled_t16[:, 1, :, :], scaled_t[:, :, :], RS, scaled_t16[:, 0, :, :],
                                                       ALU.mult, ALU.subtract).then_inc(s.split_set, 1)
                        dve.wait_ge(s.split_set, b * 8 + (2 * pair + 2))
                        for x in range(2):
                            nc.vector.transpose(res16[:, x, pair // 2, pair % 2, :],
                                                scaled_t16[:, x, :, :].rearrange("p c r -> p (c r)")).then_inc(s.res_set, 1)

                def combine(b, k, bank):
                    dve.wait_ge(s.pe_done[PROJ], b * 4 + (k + 1))
                    wait(dve, s.comb_set, b * 4 + k)
                    for t in range(2):
                        here = slice(t * D, (t + 1) * D)
                        if exact:
                            ins = nc.vector.tensor_tensor(s_b[:, here], bank[:, here], b_p[:, :], ALU.add)
                        else:
                            ins = nc.vector.scalar_tensor_tensor(s_b[:, here], bank[:, here], 1.0 / (RS * WS), b_p[:, :], ALU.mult, ALU.add)
                    ins.then_inc(s.s_set, 1)
                    dve.wait_ge(s.s_set, b * 4 + (k + 1))
                    dve.wait_ge(s.gate_set, b * 4 + (k + 1))
                    nc.vector.scalar_tensor_tensor(s_b[:, :], s_b[:, :], 0.5 / SPIKE_STEPS, cnt[:, k, :],
                                                   ALU.mult, ALU.mult).then_inc(s.comb_link, 1)
                    dve.wait_ge(s.comb_link, b * 4 + (k + 1))
                    dve.wait_ge(s.x_again, b * 32 + 16 * (k // 2 + 1))
                    tiles = slice(2 * (k % 2), 2 * (k % 2) + 2)
                    nc.vector.tensor_tensor(x_out[:, tiles, :], s_b[:, :].rearrange("p (t d) -> p t d", t=2),
                                            x_out[:, tiles, :], ALU.add).then_inc(s.comb_set, 1)

                def row_maxima(b):
                    wait(dve, s.max_t, b)
                    for i in range(H * TT):
                        dve.wait_ge(s.max_scored, b * 128 + (i + 1))
                        nc.vector.tensor_reduce(row_max[:, i // TT, i % TT:i % TT + 1],
                                                scores[i % 2][:, :, :].rearrange("p a n -> p (a n)"), AX.X, ALU.max) \
                            .then_inc(s.max_set, 1)
                    dve.wait_ge(s.max_t, b + 1)
                    wait(dve, s.max_out, b * 16)
                    nc.vector.tensor_scalar(row_max_t, scores[0][:, 0, 0:P], -1.0, None, ALU.mult).then_inc(s.max_set, 1)

                def reduce_bounds():
                    dve.wait_ge(squared, 4)
                    nc.vector.tensor_reduce(row_norms[:, :], fc_rows[:, :, :], AX.X, ALU.add).then_inc(used_set, 1)
                    nc.vector.tensor_reduce(used[:, 1:2], proj_again[:, :, :].rearrange("p k f -> p (k f)"), AX.X, ALU.max).then_inc(used_set, 1)
                    nc.vector.tensor_reduce(used[:, 2:3], wq_squares, AX.X, ALU.max).then_inc(used_set, 1)
                    nc.vector.tensor_reduce(used[:, 3:4], wp_again, AX.X, ALU.max).then_inc(used_set, 1)
                    dve.wait_ge(used_set, 5)
                    nc.vector.tensor_reduce(used[:, 0:1], row_norms[:, :], AX.X, ALU.max).then_inc(used_set, 1)
                    dve.wait_ge(used_set, 6)
                    nc.vector.tensor_scalar(used[:, 0:1], used[:, 0:1], 1.0 / W2MAX, None, ALU.mult).then_inc(used_set, 1)
                    nc.vector.tensor_scalar(used[:, 1:4], used[:, 1:4], 1.0 / (WMAX * WMAX), None, ALU.mult).then_inc(used_set, 1)
                    dve.wait_ge(s.min_set, B * 2)
                    nc.vector.tensor_scalar(used[0:H, 4:5], c_min[:, 0:1], -CROW / (QS * QS * (R2MAX + SHIFT)), None, ALU.mult) \
                        .then_inc(used_set, 1)
                    dve.wait_ge(used_set, 9)
                    nc.vector.tensor_reduce(used_most[:, :], used[:, :], AX.X, ALU.max).then_inc(used_set, 1)

                def set_flag():
                    dve.wait_ge(flag_in, 16)
                    nc.vector.tensor_reduce(used_all[:, 0:1], used_all, AX.X, ALU.max).then_inc(flag_part, 1)
                    dve.wait_ge(flag_part, 1)
                    nc.vector.tensor_scalar(flag[:, :], used_all[:, 0:1], 1.0, None, ALU.is_gt).then_inc(flag_set, 1)

                if exact:
                    for stack in q_rows:
                        nc.vector.memset(stack[0:33, :, :], 0.0).then_inc(cleared, 1)
                    nc.vector.memset(pick_max, 0.0).then_inc(cleared, 1)
                    dve.wait_ge(cleared, 3)
                    nc.vector.memset(pick_max[32:33, :], 1.0).then_inc(cleared, 1)
                for t in range(TT):
                    ln_stats(0, t)
                for t in range(TT):
                    ln_apply(0, t)
                if not exact:
                    dve.wait_ge(wq_split, 1)
                    nc.vector.scalar_tensor_tensor(w_q16[:, 1, :, :], w_q[:, :, :], WS, w_q16[:, 0, :, :],
                                                   ALU.mult, ALU.subtract).then_inc(wq_split, 1)
                for n, (kind, k) in enumerate(prep_groups(exact)):
                    if kind == XT and not exact:
                        x_lo(0, k, aux[n % 2])
                    if kind == Q:
                        q_split(0, k, aux[n % 2])
                    if kind == C:
                        dve.wait_ge(c_init, 1)
                        c_rows(0, k, aux[n % 2])
                if not exact:
                    split_lo(w_fc16, fc_stage, fc_split)

                def body(b, first, last):
                    groups = batch_groups(first, last, exact)
                    _, done = schedule(groups)
                    fc_pause = done[groups.index((0, FC, 7))] + 1
                    if exact:
                        row_maxima(b)
                    tasks = []
                    for n, (offset, kind, k) in enumerate(groups):
                        at, bank = done[n], aux[n % 2]
                        if kind == FC:
                            tasks.append((at, n, relu, (b, k, bank)))
                        if kind == Y:
                            tasks.append((at, n, spikes, (b, k)))
                            if k < 3:
                                tasks.append((min(at + 4, STEPS), n, gate, (b, k)))
                        if kind == PROJ:
                            tasks.append((at, n, combine, (b + offset, k, bank)))
                        if kind == XT and not exact:
                            tasks.append((at, n, x_lo, (b + 1, k, bank)))
                        if kind == Q:
                            tasks.append((at, n, q_split, (b + 1, k, bank)))
                        if kind == C:
                            tasks.append((at, n, c_rows, (b + 1, k, bank)))
                    if not last:
                        for t in range(TT):
                            tasks.append((12 + t, -1, ln_stats, (b + 1, t)))
                            tasks.append((24 + t, -1, ln_apply, (b + 1, t)))
                    elif not exact:
                        tasks.append((fc_pause + 5, -1, reduce_bounds, ()))
                        tasks.append((fc_pause + 9, -1, set_flag, ()))
                    if not first:
                        tasks.append((0, -1, normalise, (b - 1, UNITS - 1)))
                        tasks.append((3, -1, gate, (b - 1, 3)))
                    elif not exact:
                        tasks.append((2, -1, split_lo, (w_proj16, proj_stage, proj_split)))
                        tasks.append((2, 0, split_lo, (w_p16, wp_stage, wp_split)))
                    for unit in range(UNITS - 1):
                        tasks.append((TT * (unit + 1), 100, normalise, (b, unit)))
                    for _, _, task, args in sorted(tasks, key=lambda task: task[:2]):
                        task(*args)

                batches(dve, body)
                normalise(B - 1, UNITS - 1)
                gate(B - 1, 3)
                for n, (kind, k) in enumerate(TAIL):
                    combine(B - 1, k, aux[n])

            run(bounded, False)
            in_general(dve, run)

        @block.gpsimd
        def _(pool):
            nc.gpsimd.memset(v_ones[:, :, :, :], 1.0).then_inc(v_set, 1)
            pool.wait_ge(v_set, 1)
            nc.gpsimd.memset(key_row[:, H // 2:, :], TWO_CROW).then_inc(v_set, 1)
            pool.wait_ge(v_set, 2)

            def run(s, exact):
                def inv_std(b):
                    wait(pool, s.xn_set, b * 8)
                    wait_apart(pool, s.aggr_set, b * 8 + 8)
                    nc.gpsimd.tensor_scalar(var_eps[:, :], mean_var[:, :, 1], LN_EPS, None, ALU.add).then_inc(s.veps_set, 1)
                    pool.wait_ge(s.veps_set, b + 1)
                    nc.gpsimd.tensor_tensor(rstd[:, :], var_eps[:, :], minus_half[:, :], ALU.pow).then_inc(s.rstd_set, 1)

                def square_q(b, k):
                    chunk, half = k % 2, k // 2
                    cols = slice(half * HALF, (half + 1) * HALF)
                    pool.wait_ge(s.qhi_set, b * 4 + (k + 1))
                    wait(pool, s.pe_done[C], b * 2)
                    nc.gpsimd.tensor_tensor(q_sq[:, chunk, cols], q_hi[:, chunk, cols], q_hi[:, chunk, cols], ALU.mult).then_inc(s.sq_set, 1)

                def place_v(b, g):
                    wait(pool, s.pv_done, (b - 1) * 64 + (NG + g + 1) * TT)
                    wait_apart(pool, s.v_staged, b * 4 + 4)
                    at = 16 * (g % 2)
                    nc.gpsimd.tensor_copy(v_ones[:, :, G * g:G * g + G, at:at + DH],
                                          v_stage[:, :, G * g * DH:(G * g + G) * DH].rearrange("p t (h e) -> p t h e", h=G)).then_inc(s.vones_set, 1)

                def square_h(b, k):
                    f = k % KF
                    pool.wait_ge(s.relu_set, b * 16 + (k + 1))
                    wait(pool, s.pe_done[Y], b * 4 + (2 * (k // KF)))
                    tile = r[:, k % 2, :]
                    if exact:
                        nc.gpsimd.tensor_tensor(h_t[:, f, :], tile, tile, ALU.mult).then_inc(s.h_set, 1)
                        return
                    wait(pool, s.h_set, b * 16 + k)
                    nc.gpsimd.tensor_tensor(r_squared[:, :], tile, tile, ALU.mult).then_inc(s.rsq_set, 1)
                    pool.wait_ge(s.hhi_set, b * 16 + (k + 1))
                    pool.wait_ge(s.rsq_set, b * 16 + (k + 1))
                    nc.gpsimd.tensor_tensor(h_t16[:, 1, f, :], r_squared[:, :], h_t16[:, 0, f, :], ALU.subtract).then_inc(s.h_set, 1)

                def square_weights():
                    pool.wait_ge(checks_in, 3 * 16)
                    pool.wait_ge(s.q_out, B * 64)
                    pool.wait_ge(s.sq_set, B * 4)
                    for squares, w in ((fc_rows[:, :, :], fc_rows[:, :, :]), (proj_again[:, :, :], proj_again[:, :, :]),
                                       (wp_again, wp_again),
                                       (wq_squares, w_q[:, :, :].rearrange("p k f -> p (k f)"))):
                        nc.gpsimd.tensor_tensor(squares, w, w, ALU.mult).then_inc(squared, 1)

                pool.wait_ge(w_set, 2)
                inv_std(0)
                if not exact:
                    for k in range(4):
                        square_q(0, k)
                for g in range(NG):
                    place_v(0, g)

                def body(b, first, last):
                    groups = batch_groups(first, last, exact)
                    _, done = schedule(groups)
                    tasks = []
                    for n, (offset, kind, k) in enumerate(groups):
                        if kind == FC:
                            tasks.append((done[n], square_h, (b, k)))
                        if kind == Q and not exact:
                            tasks.append((done[n], square_q, (b + 1, k)))
                        if (kind, k) == (V, 3):
                            tasks += [(max(done[n] + 1, TT * (NG + g + 1)), place_v, (b + 1, g)) for g in range(NG)]
                    if not last:
                        tasks.append((20, inv_std, (b + 1,)))
                    elif not exact:
                        tasks.append((done[groups.index((0, FC, 7))] + 1, square_weights, ()))
                    for _, task, args in sorted(tasks, key=lambda task: task[0]):
                        task(*args)

                batches(pool, body)

            run(bounded, False)
            in_general(pool, run)


def kernel(L0_attn_x, L0_attn_Wq, L0_attn_Wp, L0_attn_bp, L0_ffn_W_fc, L0_ffn_W_proj):
    import numpy as np
    import concourse.bacc as bacc
    from concourse.bass_utils import run_bass_kernel_spmd

    x, wq, wp, bp, wfc, wproj = (np.asarray(a) for a in (L0_attn_x, L0_attn_Wq, L0_attn_Wp, L0_attn_bp, L0_ffn_W_fc, L0_ffn_W_proj))
    wp_rows = wp.T.reshape(NG // 2, 2, G, DH, D)
    wp_s = wp_rows.transpose(2, 1, 3, 0, 4).reshape(P, NG // 2, D)
    ident = np.eye(P, dtype=np.float32)
    p = np.arange(P)
    head_sum = np.zeros((P, KD, H), np.float32)
    for k in range(KD):
        head_sum[p, k, 8 * k + p // DH] = 1.0
    arrays = {
        "x": x, "wq_t": wq.transpose(0, 2, 1), "wp_s": wp_s, "bp": bp,
        "wfc_t": wfc.T.reshape(KD, P, F).transpose(1, 0, 2),
        "wfc_rows": wfc,
        "wproj_t": wproj.T.reshape(KF, P, D).transpose(1, 0, 2),
        "consts": np.concatenate([ident, head_sum.reshape(P, -1)], 1),
    }
    arrays = {k: np.ascontiguousarray(v) for k, v in arrays.items()}
    nc = bacc.Bacc("TRN2", target_bir_lowering=False, num_devices=1)
    args = {k: nc.dram_tensor(k, v.shape, FP32, kind="ExternalInput").ap() for k, v in arrays.items()}
    q_scratch = nc.dram_tensor("q_scratch", (H, 2, DH, N), FP16, kind="Internal").ap()
    c_scratch = nc.dram_tensor("c_scratch", (H, N), FP16, kind="Internal").ap()
    q_own_scratch = nc.dram_tensor("q_own_scratch", (H, DH, N), FP32, kind="Internal").ap()
    max_scratch = nc.dram_tensor("max_scratch", (P, P), FP32, kind="Internal").ap()
    bound_scratch = nc.dram_tensor("bound_scratch", (P, 1), FP32, kind="Internal").ap()
    out = nc.dram_tensor("out", (B, N, D), FP32, kind="ExternalOutput").ap()
    build(nc, **args, q_scratch=q_scratch, c_scratch=c_scratch, q_own_scratch=q_own_scratch,
          max_scratch=max_scratch, bound_scratch=bound_scratch, out=out)
    got = run_bass_kernel_spmd(nc, [arrays], core_ids=[0])
    return got.results[0]["out"]
```
